# Optimizing a Trainium2 kernel written in Bass

```python
import numpy as np
import jax
import jax.numpy as jnp

def _softmax(x, axis=-1):
    return jax.nn.softmax(x, axis=axis)

def _gelu(x):
    return jax.nn.gelu(x, approximate=True)

def _silu(x):
    return jax.nn.silu(x)

def _sigmoid(x):
    return jax.nn.sigmoid(x)

def _layernorm(x, axis=-1, eps=1e-05):
    m = jnp.mean(x, axis=axis, keepdims=True)
    v = jnp.var(x, axis=axis, keepdims=True)
    return (x - m) / jnp.sqrt(v + eps)

def _scatter_add(tgt, idx, src, axis=0):
    return tgt.at[idx].add(src)

def _segment_sum(src, seg, n):
    return jax.ops.segment_sum(src, seg, n)
kernel_name = 'mk_gnn_resnorm_d4_gnn_r8_e21d37'

def setup_inputs(seed: int=0):
    np.random.seed(seed)
    _w = jnp.asarray

    def _rec_inputs():
        import jax
        import jax.numpy as jnp
        _gk = jax.random.key(seed)
        x = -0.0001006 + 1 * jax.random.normal(jax.random.fold_in(_gk, 1), (6250, 96), jnp.float32)
        _s = jax.random.randint(jax.random.fold_in(_gk, 2), (100000,), 0, 6250, jnp.int32)
        _d = jax.random.randint(jax.random.fold_in(_gk, 3), (100000,), 0, 6250, jnp.int32)
        _loop = jnp.arange(6250, dtype=jnp.int32)
        src = jnp.concatenate([_s, _d, _loop])
        dst = jnp.concatenate([_d, _s, _loop])
        _o = jnp.argsort(dst, stable=True)
        src = src[_o]
        dst = dst[_o]
        edge_attr_96 = 5.93493e-05 + 1.00006 * jax.random.normal(jax.random.fold_in(_gk, 11), (206250, 96), jnp.float32)
        return (x, src, dst, edge_attr_96)
    x, src, dst, edge_attr_96 = _rec_inputs()

    def _L0_gnn_setup():
        import jax, jax.numpy as jnp
        import numpy as np
        N_NODES = 6250
        N_EDGES = 100000
        IN_DIM = 96
        NUM_HEADS = 8
        HEAD_DIM = IN_DIM // NUM_HEADS
        key = jax.random.key(seed)
        ks = jax.random.split(key, 11)
        s = 1.0 / np.sqrt(IN_DIM)
        return {'x': jax.random.normal(ks[0], (N_NODES, IN_DIM), dtype=jnp.float32), 'edge_index': jax.random.randint(ks[1], (2, N_EDGES), 0, N_NODES, dtype=jnp.int64), 'edge_attr': jax.random.normal(ks[2], (N_EDGES, IN_DIM), dtype=jnp.float32), 'Wq': jax.random.normal(ks[3], (IN_DIM, IN_DIM), dtype=jnp.float32) * s, 'bq': jax.random.normal(ks[4], (IN_DIM,), dtype=jnp.float32) * s, 'Wk': jax.random.normal(ks[5], (IN_DIM, IN_DIM), dtype=jnp.float32) * s, 'bk': jax.random.normal(ks[6], (IN_DIM,), dtype=jnp.float32) * s, 'We': jax.random.normal(ks[7], (IN_DIM, IN_DIM), dtype=jnp.float32) * s, 'be': jax.random.normal(ks[8], (IN_DIM,), dtype=jnp.float32) * s, 'Wv': jax.random.normal(ks[9], (IN_DIM, IN_DIM), dtype=jnp.float32) * s, 'bv': jax.random.normal(ks[10], (IN_DIM,), dtype=jnp.float32) * s}
    _L0_gnn_all = _L0_gnn_setup()
    _L0_gnn_in = {k: v for k, v in _L0_gnn_all.items() if k in ('Wq', 'bq', 'Wk', 'bk', 'We', 'be', 'Wv', 'bv')}
    del _L0_gnn_all

    def _L1_gnn_setup():
        import jax, jax.numpy as jnp
        import numpy as np
        BN_EPS = 1e-05
        key = jax.random.key(seed)
        ks = jax.random.split(key, 5)
        N, E, D = (6250, 100000, 96)
        x = jax.random.normal(ks[0], (N, D), dtype=jnp.float32)
        edge_index = jax.random.randint(ks[1], (2, E), 0, N, dtype=jnp.int64)
        Wl = jax.random.normal(ks[2], (D, D), dtype=jnp.float32) / np.sqrt(D)
        bl = jnp.zeros((D,), dtype=jnp.float32)
        Wr = jax.random.normal(ks[3], (D, D), dtype=jnp.float32) / np.sqrt(D)
        gamma = jnp.ones((D,), dtype=jnp.float32)
        beta = jnp.zeros((D,), dtype=jnp.float32)
        return {'x': x, 'edge_index': edge_index, 'Wl': Wl, 'bl': bl, 'Wr': Wr, 'gamma': gamma, 'beta': beta}
    _L1_gnn_all = _L1_gnn_setup()
    _L1_gnn_in = {k: v for k, v in _L1_gnn_all.items() if k in ('Wl', 'bl', 'Wr', 'gamma', 'beta')}
    del _L1_gnn_all

    def _L2_gnn_setup():
        import jax, jax.numpy as jnp
        import numpy as np
        N = 6250
        E = 100000
        IN = 96
        H = 96
        OUT = 96

        def _gcn(x, W, b, src, dst, norm, n):
            h = x @ W
            msg = h[src] * norm[:, None]
            out = jax.ops.segment_sum(msg, dst, num_segments=n)
            return out + b
        key = jax.random.key(seed)
        ks = jax.random.split(key, 12)
        s = 1.0 / np.sqrt(IN)
        sh = 1.0 / np.sqrt(H)
        return {'x': jax.random.normal(ks[0], (N, IN), dtype=jnp.float32), 'edge_index': jax.random.randint(ks[1], (2, E), 0, N, dtype=jnp.int32), 'W_local': jax.random.uniform(ks[2], (IN, H), jnp.float32, -s, s), 'b_local': jnp.zeros((H,), jnp.float32), 'W_g1': jax.random.uniform(ks[3], (IN, H), jnp.float32, -s, s), 'b_g1': jnp.zeros((H,), jnp.float32), 'W_g2': jax.random.uniform(ks[4], (H, H), jnp.float32, -sh, sh), 'b_g2': jnp.zeros((H,), jnp.float32), 'W_fuse': jax.random.uniform(ks[5], (2 * H, OUT), jnp.float32, -1.0 / np.sqrt(2 * H), 1.0 / np.sqrt(2 * H)), 'b_fuse': jnp.zeros((OUT,), jnp.float32)}
    _L2_gnn_all = _L2_gnn_setup()
    _L2_gnn_in = {k: v for k, v in _L2_gnn_all.items() if k in ('W_local', 'b_local', 'W_g1', 'b_g1', 'W_g2', 'b_g2', 'W_fuse', 'b_fuse')}
    del _L2_gnn_all

    def _L3_gnn_setup():
        import jax, jax.numpy as jnp
        import numpy as np
        N_NODES = 6250
        N_EDGES = 100000
        DIM = 96
        key = jax.random.key(seed)
        k = jax.random.split(key, 6)
        x = jax.random.normal(k[0], (N_NODES, DIM), dtype=jnp.float32)
        edge_index = jax.random.randint(k[1], (2, N_EDGES), 0, N_NODES, dtype=jnp.int64)
        edge_attr = jax.random.normal(k[2], (N_EDGES, DIM), dtype=jnp.float32)
        scale = 1.0 / np.sqrt(DIM)
        W1 = jax.random.normal(k[3], (DIM, DIM), dtype=jnp.float32) * scale
        b1 = jnp.zeros((DIM,), dtype=jnp.float32)
        W2 = jax.random.normal(k[4], (DIM, DIM), dtype=jnp.float32) * scale
        b2 = jnp.zeros((DIM,), dtype=jnp.float32)
        return {'x': x, 'edge_index': edge_index, 'edge_attr': edge_attr, 'W1': W1, 'b1': b1, 'W2': W2, 'b2': b2}
    _L3_gnn_all = _L3_gnn_setup()
    _L3_gnn_in = {k: v for k, v in _L3_gnn_all.items() if k in ('W1', 'b1', 'W2', 'b2')}
    del _L3_gnn_all
    return {'x': x, 'src': src, 'dst': dst, 'edge_attr_96': edge_attr_96, 'L0_gnn_Wq': _L0_gnn_in['Wq'], 'L0_gnn_bq': _L0_gnn_in['bq'], 'L0_gnn_Wk': _L0_gnn_in['Wk'], 'L0_gnn_bk': _L0_gnn_in['bk'], 'L0_gnn_We': _L0_gnn_in['We'], 'L0_gnn_be': _L0_gnn_in['be'], 'L0_gnn_Wv': _L0_gnn_in['Wv'], 'L0_gnn_bv': _L0_gnn_in['bv'], 'L1_gnn_Wl': _L1_gnn_in['Wl'], 'L1_gnn_bl': _L1_gnn_in['bl'], 'L1_gnn_Wr': _L1_gnn_in['Wr'], 'L1_gnn_gamma': _L1_gnn_in['gamma'], 'L1_gnn_beta': _L1_gnn_in['beta'], 'L2_gnn_W_local': _L2_gnn_in['W_local'], 'L2_gnn_b_local': _L2_gnn_in['b_local'], 'L2_gnn_W_g1': _L2_gnn_in['W_g1'], 'L2_gnn_b_g1': _L2_gnn_in['b_g1'], 'L2_gnn_W_g2': _L2_gnn_in['W_g2'], 'L2_gnn_b_g2': _L2_gnn_in['b_g2'], 'L2_gnn_W_fuse': _L2_gnn_in['W_fuse'], 'L2_gnn_b_fuse': _L2_gnn_in['b_fuse'], 'L3_gnn_W1': _L3_gnn_in['W1'], 'L3_gnn_b1': _L3_gnn_in['b1'], 'L3_gnn_W2': _L3_gnn_in['W2'], 'L3_gnn_b2': _L3_gnn_in['b2']}

def reference(x, src, dst, edge_attr_96, L0_gnn_Wq, L0_gnn_bq, L0_gnn_Wk, L0_gnn_bk, L0_gnn_We, L0_gnn_be, L0_gnn_Wv, L0_gnn_bv, L1_gnn_Wl, L1_gnn_bl, L1_gnn_Wr, L1_gnn_gamma, L1_gnn_beta, L2_gnn_W_local, L2_gnn_b_local, L2_gnn_W_g1, L2_gnn_b_g1, L2_gnn_W_g2, L2_gnn_b_g2, L2_gnn_W_fuse, L2_gnn_b_fuse, L3_gnn_W1, L3_gnn_b1, L3_gnn_W2, L3_gnn_b2):
    import jax
    import jax.numpy as jnp

    def _L0_gnn_ref(x, edge_index, edge_attr, Wq, bq, Wk, bk, We, be, Wv, bv):
        import jax, jax.numpy as jnp
        import numpy as np
        N_NODES = 6250
        N_EDGES = 100000
        IN_DIM = 96
        NUM_HEADS = 8
        HEAD_DIM = IN_DIM // NUM_HEADS
        N = x.shape[0]
        H, D = (NUM_HEADS, HEAD_DIM)
        Q_h = (x @ Wq + bq).reshape(N, H, D)
        K_h = (x @ Wk + bk).reshape(N, H, D)
        V_h = (x @ Wv + bv).reshape(N, H, D)
        E = (edge_attr @ We + be).reshape(-1, H, D)
        src_idx = edge_index[0]
        dst_idx = edge_index[1]
        src = K_h[src_idx]
        dest = Q_h[dst_idx]
        score = src * dest / jnp.sqrt(jnp.asarray(D, x.dtype))
        score = score * E
        score = jnp.exp(jnp.clip(score.sum(-1, keepdims=True), -5.0, 5.0))
        msg = V_h[src_idx] * score
        wV = jax.ops.segment_sum(msg, dst_idx, num_segments=N)
        Z = jax.ops.segment_sum(score, dst_idx, num_segments=N)
        h_out = wV / (Z + 1e-06)
        return h_out.reshape(N, H * D)

    def _L1_gnn_ref(x, edge_index, Wl, bl, Wr, gamma, beta):
        import jax, jax.numpy as jnp
        import numpy as np
        BN_EPS = 1e-05
        N = x.shape[0]
        src, dst = (edge_index[0], edge_index[1])
        msg_sum = jax.ops.segment_sum(x[src], dst, num_segments=N)
        deg = jax.ops.segment_sum(jnp.ones_like(src, dtype=x.dtype), dst, num_segments=N)
        neigh_mean = msg_sum / jnp.maximum(deg, 1.0)[:, None]
        h = jnp.einsum('nd,od->no', neigh_mean, Wl) + bl + jnp.einsum('nd,od->no', x, Wr)
        mu = h.mean(axis=0)
        var = h.var(axis=0)
        h = (h - mu) * jax.lax.rsqrt(var + BN_EPS) * gamma + beta
        return jax.nn.relu(h)

    def _L2_gnn_ref(x, edge_index, W_local, b_local, W_g1, b_g1, W_g2, b_g2, W_fuse, b_fuse):
        import jax, jax.numpy as jnp
        import numpy as np
        N = 6250
        E = 100000
        IN = 96
        H = 96
        OUT = 96

        def _gcn(x, W, b, src, dst, norm, n):
            h = x @ W
            msg = h[src] * norm[:, None]
            out = jax.ops.segment_sum(msg, dst, num_segments=n)
            return out + b
        n = x.shape[0]
        loops = jnp.arange(n, dtype=edge_index.dtype)
        src = jnp.concatenate([edge_index[0], loops])
        dst = jnp.concatenate([edge_index[1], loops])
        deg = jax.ops.segment_sum(jnp.ones_like(dst, dtype=x.dtype), dst, num_segments=n)
        dis = jax.lax.rsqrt(jnp.maximum(deg, 1.0))
        norm = dis[src] * dis[dst]
        local = jax.nn.relu(_gcn(x, W_local, b_local, src, dst, norm, n))
        g = jax.nn.relu(_gcn(x, W_g1, b_g1, src, dst, norm, n))
        g = jax.nn.relu(_gcn(g, W_g2, b_g2, src, dst, norm, n))
        combined = jnp.concatenate([local, g], axis=-1)
        return combined @ W_fuse + b_fuse

    def _L3_gnn_ref(x, edge_index, edge_attr, W1, b1, W2, b2):
        import jax, jax.numpy as jnp
        import numpy as np
        N_NODES = 6250
        N_EDGES = 100000
        DIM = 96
        src = edge_index[0]
        dst = edge_index[1]
        msg = jax.nn.relu(x[src] + edge_attr)
        aggr = jax.ops.segment_sum(msg, dst, num_segments=x.shape[0])
        h = x + aggr
        h = jax.nn.relu(h @ W1 + b1) @ W2 + b2
        return x + jax.nn.relu(h)
    edge_index = jnp.stack([src, dst])
    x = _layernorm(x + _L0_gnn_ref(x, edge_index, edge_attr_96, L0_gnn_Wq, L0_gnn_bq, L0_gnn_Wk, L0_gnn_bk, L0_gnn_We, L0_gnn_be, L0_gnn_Wv, L0_gnn_bv), axis=-1)
    x = _layernorm(x + _L1_gnn_ref(x, edge_index, L1_gnn_Wl, L1_gnn_bl, L1_gnn_Wr, L1_gnn_gamma, L1_gnn_beta), axis=-1)
    x = _layernorm(x + _L2_gnn_ref(x, edge_index, L2_gnn_W_local, L2_gnn_b_local, L2_gnn_W_g1, L2_gnn_b_g1, L2_gnn_W_g2, L2_gnn_b_g2, L2_gnn_W_fuse, L2_gnn_b_fuse), axis=-1)
    x = _layernorm(x + _L3_gnn_ref(x, edge_index, edge_attr_96, L3_gnn_W1, L3_gnn_b1, L3_gnn_W2, L3_gnn_b2), axis=-1)
    return x

_drawn_inputs = setup_inputs


def setup_inputs(seed=0):
    import zlib

    import numpy as np

    out = dict(_drawn_inputs(seed))
    spreads = {'L1_gnn_bl': (0.0, 2.0),
     'L1_gnn_gamma': (1.0, 0.2),
     'L1_gnn_beta': (0.0, 0.1),
     'L2_gnn_b_local': (0.0, 0.364),
     'L2_gnn_b_g1': (0.0, 0.582),
     'L2_gnn_b_g2': (0.0, 0.307),
     'L2_gnn_b_fuse': (0.0, 0.1),
     'L3_gnn_b1': (0.0, 0.8),
     'L3_gnn_b2': (0.0, 0.781)}
    factors = {'L0_gnn_bq': 4.475,
     'L0_gnn_bk': 4.646,
     'L0_gnn_be': 3.821,
     'L2_gnn_W_g1': 5.49,
     'L2_gnn_W_g2': 3.213}
    for name, (base, spread) in spreads.items():
        noise = np.random.default_rng([zlib.crc32(name.encode()), seed]).standard_normal(out[name].shape)
        drawn = base * np.exp(spread * noise) if base else spread * noise
        out[name] = jnp.asarray(drawn.astype(out[name].dtype))
    for name, factor in factors.items():
        out[name] = (out[name] * factor).astype(out[name].dtype)
    return out
```

```python
from contextlib import ExitStack

import concourse.bass as bass
from concourse import mybir

ALU = mybir.AluOpType
ACT = mybir.ActivationFunctionType
AX_X = mybir.AxisListType.X
F32 = mybir.dt.float32
I32 = mybir.dt.int32
ds = bass.ds

P = 128
N = 6250
D = 96
E = 206250
H = 8
HD = D // H
COLS = 8
EPB = P * COLS
NB = -(-E // EPB)
NB += NB % 2
PAIRS = NB // 2
FULL = E // EPB
REST = E - FULL * EPB
WIN = 48
ROUNDS = -(-N // WIN)
SUB = COLS // 2
MROWS = D + H + 1
NPAD = N + WIN
TN = 125
TILES = N // TN
ST = 5
STEPS = TILES // ST
SN = ST * TN
CUT = 4 * TN
PIECES = ((0, 0, CUT), (CUT, 512, SN - CUT))
GATHERED = 16 * COLS
EPS = 1e-5
CLIP = 5.0 * HD ** 0.5


def semaphores(nc, ctx, names, tag):
    return {n: ctx.enter_context(nc.semaphore(f"{tag}_{n}")) for n in names}


def clear_semaphores(nc, s):
    with nc.Block() as block:
        @block.vector
        def _(dve):
            for sem in s.values():
                dve.sem_clear(sem)


def sbuf(nc, name, shape, dt):
    return nc.sbuf_tensor(f"{name}_{nc.next_id()}", shape, dt)


def psum(nc, name, shape, dt):
    return nc.psum_tensor(f"{name}_{nc.next_id()}", shape, dt)


def wait(eng, sem, count):
    if not (isinstance(count, int) and count == 0):
        eng.wait_ge(sem, count)


def steps(eng, turn):
    turn(0)
    with eng.Fori(1, STEPS) as t:
        turn(t)


class Chain:

    def __init__(self, eng, sem, turn=0, per=0):
        self.eng, self.sem, self.turn, self.per, self.n = eng, sem, turn, per, 0

    def then(self, ins):
        ins.then_inc(self.sem, 1)
        self.n += 1
        self.eng.wait_ge(self.sem, self.turn * self.per + self.n)


def setup(nc, c, A):
    with ExitStack() as ctx:
        s = semaphores(nc, ctx, ["loaded", "made", "chain", "iota_made", "counted", "bases", "summed", "padded"], "setup")
        iota_i = ctx.enter_context(sbuf(nc, "iota_i", [P, WIN], I32))
        dst_i = ctx.enter_context(sbuf(nc, "dst_i", [P, NB * COLS], I32))
        inside = ctx.enter_context(sbuf(nc, "inside", [P, NB * COLS], F32))
        first_row = ctx.enter_context(sbuf(nc, "first_row", [P, P], F32))
        ones = ctx.enter_context(sbuf(nc, "ones", [P, P], F32))
        count = ctx.enter_context(sbuf(nc, "count", [P, 4], F32))
        zero = ctx.enter_context(sbuf(nc, "zero", [WIN, D], F32))
        ps = ctx.enter_context(psum(nc, "setup_ps", [P, 512], F32))
        with nc.Block() as block:
            @block.sync
            def _(sp):
                loads = [
                    (dst_i[:, :], A["dst"].rearrange("b p g -> p b g")),
                    (c.x_nodes[:, :, :], A["x"].rearrange("(t p) f -> p t f", p=TN)),
                    (c.w_kvq[0:D, 0, :], A["L0_gnn_Wk"]), (c.w_kvq[D:D + 1, 0, :], A["L0_gnn_bk"]),
                    (c.w_kvq[0:D, 1, :], A["L0_gnn_Wv"]), (c.w_kvq[D:D + 1, 1, :], A["L0_gnn_bv"]),
                    (c.w_kvq[0:D, 2, :], A["L0_gnn_Wq"]), (c.w_kvq[D:D + 1, 2, :], A["L0_gnn_bq"]),
                    (c.w_e[0:D, :], A["L0_gnn_We"]), (c.w_e[D:D + 1, :], A["L0_gnn_be"]),
                    (c.w_l[:, :], A["L1_gnn_WlT"]), (c.w_r[:, :], A["L1_gnn_WrT"]),
                    (c.w_local[:, :], A["L2_gnn_W_local"]), (c.w_g1[:, :], A["L2_gnn_W_g1"]),
                    (c.w_g2[:, :], A["L2_gnn_W_g2"]),
                    (c.w_f1[0:D, :], A["L2_gnn_W_fuse"][0:D, :]), (c.w_f1[D:D + 1, :], A["L2_gnn_b_fuse"]),
                    (c.w_f2[:, :], A["L2_gnn_W_fuse"][D:2 * D, :]),
                    (c.w_1[:, :], A["L3_gnn_W1"]),
                    (c.w_2[0:D, :], A["L3_gnn_W2"]), (c.w_2[D:D + 1, :], A["L3_gnn_b2"]),
                    (c.b_l[:, :], A["L1_gnn_bl"]), (c.gamma[:, :], A["L1_gnn_gamma"]),
                    (c.beta[:, :], A["L1_gnn_beta"]), (c.b_local[:, :], A["L2_gnn_b_local"]),
                    (c.b_g1[:, :], A["L2_gnn_b_g1"]), (c.b_g2[:, :], A["L2_gnn_b_g2"]),
                    (c.b_1[:, :], A["L3_gnn_b1"]),
                ]
                for to, of in loads:
                    sp.dma_start(to, of).then_inc(s["loaded"], 16)
                sp.wait_ge(s["loaded"], 16 * len(loads))
                sp.sem_inc(s["counted"], 1)
                sp.wait_ge(s["padded"], 1)
                sp.dma_start(c.q_table[N:NPAD, :], zero[:, :]).then_inc(s["loaded"], 16)
                sp.wait_ge(s["loaded"], 16 * len(loads) + 16)

            @block.gpsimd
            def _(pool):
                pool.iota(iota_i[:, :], pattern=[[1, WIN]], base=0, channel_multiplier=0).then_inc(s["iota_made"], 1)
                pool.memset(c.ident[:, :], 0.0).then_inc(s["made"], 1)
                pool.memset(first_row[:, :], 1.0).then_inc(s["made"], 1)
                pool.memset(c.count_row[:, :], 1.0).then_inc(s["made"], 1)
                pool.wait_ge(s["made"], 3)
                pool.affine_select(out=c.ident[:, :], in_=c.ident[:, :], compare_op=ALU.not_equal, fill=1.0,
                                   base=0, pattern=[[-1, P]], channel_multiplier=1).then_inc(s["made"], 1)
                pool.affine_select(out=first_row[:, :], in_=first_row[:, :], compare_op=ALU.is_equal, fill=0.0,
                                   base=0, pattern=[[0, P]], channel_multiplier=1).then_inc(s["made"], 1)
                pool.affine_select(out=c.count_row[:, :], in_=c.count_row[:, :], compare_op=ALU.is_equal, fill=0.0,
                                   base=-(MROWS - 1), pattern=[[0, D]], channel_multiplier=1).then_inc(s["made"], 1)

            @block.vector
            def _(dve):
                dve.memset(zero[:, :], 0.0).then_inc(s["padded"], 1)
                dve.memset(ones[:, :], 1.0)
                dve.memset(c.sums[:, :], 0.0)
                dve.memset(c.eps[:, :], EPS)
                dve.memset(c.rel[:, NB * COLS:], -1.0)
                ch = Chain(dve, s["chain"])
                ch.then(dve.memset(c.round_base[:, :], 0.0))
                dve.wait_ge(s["iota_made"], 1)
                ch.then(dve.tensor_copy(c.iota[:, :], iota_i[:, :]))
                dve.wait_ge(s["counted"], 1)
                dve.tensor_copy(c.dst_f[:, :], dst_i[:, :]).then_inc(s["bases"], 1)
                dve.wait_ge(s["summed"], 1)
                ch.then(dve.tensor_copy(c.first_dst[:, :], ps[:, 0:NB]))
                rel = c.rel[:, 0:NB * COLS].rearrange("p (b g) -> p b g", g=COLS)
                ch.then(dve.tensor_tensor(rel, c.dst_f[:, :].rearrange("p (b g) -> p b g", g=COLS),
                                          c.first_dst[:, :].unsqueeze(2).to_broadcast([P, NB, COLS]), ALU.subtract))
                ch.then(dve.tensor_scalar(inside[:, :], c.rel[:, 0:NB * COLS], 0.0, None, ALU.is_ge))
                ch.then(dve.scalar_tensor_tensor(out=inside[:, :], in0=c.rel[:, 0:NB * COLS], scalar=float(WIN),
                                                 in1=inside[:, :], op0=ALU.is_lt, op1=ALU.mult))
                dve.tensor_reduce(count[:, 0:1], inside[:, :], AX_X, ALU.add).then_inc(s["bases"], 1)
                dve.wait_ge(s["summed"], 2)
                ch.then(dve.tensor_scalar(c.sorted_[:, :], ps[:, 256:257], float(E), None, ALU.is_equal))
                ch.then(dve.tensor_scalar(count[:, 1:2], c.sorted_[:, :], float(1 - ROUNDS), float(ROUNDS), ALU.mult, ALU.add))
                ch.then(dve.tensor_copy(c.n_rounds[:, :], count[:, 1:2]))

            @block.tensor
            def _(pe):
                pe.wait_ge(s["made"], 6)
                pe.wait_ge(s["bases"], 1)
                pe.matmul(ps[:, 0:NB], first_row[:, :], c.dst_f[:, :].rearrange("p (b g) -> p b g", g=COLS)[:, :, 0],
                          start=True, stop=True).then_inc(s["summed"], 1)
                pe.wait_ge(s["bases"], 2)
                pe.matmul(ps[:, 256:257], ones[:, :], count[:, 0:1], start=True, stop=True).then_inc(s["summed"], 1)
        clear_semaphores(nc, s)


def project(nc, c, A):
    with ExitStack() as ctx:
        s = semaphores(nc, ctx, ["x_loaded", "turned", "turned_copied", "multiplied", "kv_copied", "q_copied", "stored",
                           "ones_made"], "project")
        x_step = ctx.enter_context(sbuf(nc, "x_step", [TN, ST, D], F32))
        xt = ctx.enter_context(sbuf(nc, "xt", [D + 1, SN], F32))
        rows = ctx.enter_context(sbuf(nc, "rows", [TN, ST, 3 * D], F32))
        ps_t = ctx.enter_context(psum(nc, "ps_t", [P, 1024], F32))
        ps_r = ctx.enter_context(psum(nc, "ps_r", [P, ST, 512], F32))
        w = c.w_kvq[:, :, :].rearrange("k a f -> k (a f)")
        with nc.Block() as block:
            @block.sync
            def _(sp):
                def turn(t):
                    wait(sp, s["turned"], t)
                    sp.dma_start(x_step[:, :, :], A["x"].rearrange("(t k p) f -> t p k f", k=ST, p=TN)[ds(t, 1)]
                                 .rearrange("a p k f -> (a p) k f")).then_inc(s["x_loaded"], 16)
                    sp.wait_ge(s["kv_copied"], t + 1)
                    sp.dma_start(c.kv_table.rearrange("(t k p) f -> t p k f", k=ST, p=TN)[ds(t, 1)]
                                 .rearrange("a p k f -> (a p) k f"), rows[:, :, 0:2 * D]).then_inc(s["stored"], 16)
                    sp.wait_ge(s["q_copied"], t + 1)
                    sp.dma_start(c.q_table[0:N, :].rearrange("(t k p) f -> t p k f", k=ST, p=TN)[ds(t, 1)]
                                 .rearrange("a p k f -> (a p) k f"), rows[:, :, 2 * D:]).then_inc(s["stored"], 16)

                steps(sp, turn)
                sp.wait_ge(s["stored"], 32 * STEPS)

            @block.tensor
            def _(pe):
                pe.wait_ge(s["ones_made"], 1)
                def turn(t):
                    pe.wait_ge(s["x_loaded"], t * 16 + 16)
                    for k in range(ST):
                        at = k * TN if k < 4 else 512
                        ins = pe.transpose(ps_t[0:D, at:at + TN], x_step[:, k, :], c.ident[0:TN, 0:TN])
                    ins.then_inc(s["turned"], 1)
                    pe.wait_ge(s["turned_copied"], t + 1)
                    wait(pe, s["kv_copied"], t)
                    wait(pe, s["q_copied"], t)
                    for k in range(ST):
                        ins = pe.matmul(ps_r[0:TN, k, 0:3 * D], xt[:, k * TN:(k + 1) * TN], w, start=True, stop=True)
                    ins.then_inc(s["multiplied"], 1)

                steps(pe, turn)

            @block.scalar
            def _(act):
                def turn(t):
                    act.wait_ge(s["turned"], t + 1)
                    wait(act, s["multiplied"], t)
                    act.activation(xt[0:D, 0:CUT], ps_t[0:D, 0:CUT], ACT.Copy)
                    act.activation(xt[0:D, CUT:SN], ps_t[0:D, 512:512 + TN], ACT.Copy).then_inc(s["turned_copied"], 1)
                    act.wait_ge(s["multiplied"], t + 1)
                    act.wait_ge(s["kv_copied"], t + 1)
                    wait(act, s["stored"], t * 32)
                    act.activation(rows[:, :, 2 * D:], ps_r[0:TN, :, 2 * D:3 * D], ACT.Copy).then_inc(s["q_copied"], 1)

                steps(act, turn)

            @block.vector
            def _(dve):
                dve.memset(xt[D:D + 1, :], 1.0).then_inc(s["ones_made"], 1)
                def turn(t):
                    dve.wait_ge(s["multiplied"], t + 1)
                    wait(dve, s["stored"], t * 32)
                    dve.tensor_copy(rows[:, :, 0:2 * D], ps_r[0:TN, :, 0:2 * D]).then_inc(s["kv_copied"], 1)

                steps(dve, turn)
        clear_semaphores(nc, s)


def place_windows(nc, c):
    with ExitStack() as ctx:
        s = semaphores(nc, ctx, ["chain"], "windows")
        with nc.Block() as block:
            @block.vector
            def _(dve):
                ch = Chain(dve, s["chain"])
                ch.then(dve.tensor_scalar(c.base_f[:, :], c.first_dst[:, :], c.sorted_[:, 0:1], c.round_base[:, 0:1],
                                          ALU.mult, ALU.add))
                dve.tensor_copy(c.base_i[:, :], c.base_f[:, :])
                dve.tensor_tensor(c.rel[:, 0:NB * COLS].rearrange("p (b g) -> p b g", g=COLS),
                                  c.dst_f[:, :].rearrange("p (b g) -> p b g", g=COLS),
                                  c.base_f[:, :].unsqueeze(2).to_broadcast([P, NB, COLS]), ALU.subtract)
                ch.then(dve.tensor_scalar(c.round_base[:, :], c.round_base[:, :], float(WIN), None, ALU.add))
        clear_semaphores(nc, s)


def edge_pass(nc, c, A, kind, table, gathered, rnd):
    attend, relu = kind == "attend", kind == "relu"
    rows = MROWS if attend else D
    wide = 2 * D if attend else D
    names = ["idx_loaded0", "idx_loaded1", "attr_loaded0", "attr_loaded1", "q_loaded0", "q_loaded1", "onehot_made0",
             "onehot_made1", "attr_turned", "attr_copied", "onehot_turned", "onehot_copied", "turned0", "turned1",
             "eq_ready", "eq_used", "score_ready", "exp_done", "msg_made0", "msg_made1", "sum_made0", "sum_made1",
             "seg_done0", "seg_done1", "added0", "added1", "begun", "chain", "set_up"]
    with ExitStack() as outer, ExitStack() as ctx:
        s = semaphores(nc, outer, names, kind)
        outer.callback(clear_semaphores, nc, s)

        def two(name):
            return [s[name + "0"], s[name + "1"]]

        idx_loaded, attr_loaded, q_loaded, onehot_made = map(two, ("idx_loaded", "attr_loaded", "q_loaded", "onehot_made"))
        turned, msg_made, sum_made, seg_done, added = map(two, ("turned", "msg_made", "sum_made", "seg_done", "added"))

        def sb(name, shape):
            return ctx.enter_context(sbuf(nc, name, shape, F32))

        idx = ctx.enter_context(sbuf(nc, "idx", [P, 2, COLS], I32))
        got = sb("got", [P, 2, COLS, wide])
        onehot = sb("onehot", [P, 2, COLS, WIN])
        ps_seg = ctx.enter_context(psum(nc, "ps_seg", [P, 2, 512], F32))
        if kind != "plain":
            attr = sb("attr", [P, 2, COLS, D])
            msg = sb("msg", [P, 2, COLS, rows])
        if relu:
            total = sb("total", [P, 2, COLS, D])
        if attend:
            q_win = sb("q_win", [WIN, 2, D])
            attr_t = sb("attr_t", [D + 1, 2, SUB * P])
            onehot_t = sb("onehot_t", [WIN, 2, SUB * P])
            key_edge = sb("key_edge", [P, COLS, D])
            prod = sb("prod", [P, COLS, D])
            score = sb("score", [P, COLS, H])
            clipped = sb("clipped", [P, COLS, H])
            ps_at = ctx.enter_context(psum(nc, "ps_at", [P, 512], F32))
            ps_oh = ctx.enter_context(psum(nc, "ps_oh", [P, 512], F32))
            ps_e = ctx.enter_context(psum(nc, "ps_e", [P, 2, 512], F32))
            ps_q = ctx.enter_context(psum(nc, "ps_q", [P, 2, 512], F32))
        block = ctx.enter_context(nc.Block())
        src_d, attr_d = A["src"], A["edge_attr_96"]
        attr_full = attr_d[0:FULL * EPB, :].rearrange("(b p g) f -> b p (g f)", p=P, g=COLS)
        have = rnd * (PAIRS * GATHERED)

        def before(i, slot):
            return 1 - slot, (i + 1 if slot else i)

        def pairs(eng, turn):
            for i in range(2):
                for slot in range(2):
                    turn(i, slot, i == 0 and slot == 0, False)
            with eng.Fori(2, PAIRS - 1) as i:
                for slot in range(2):
                    turn(i, slot, False, False)
            for slot in range(2):
                turn(PAIRS - 1, slot, False, slot == 1)

        @block.sync
        def _(sp):
            def loads(i, slot, is_first, is_last):
                b = 2 * i + slot
                if not (isinstance(i, int) and i == 0):
                    sp.wait_ge(gathered[slot], have + i * GATHERED)
                sp.dma_start(idx[:, slot, :], src_d[ds(b, 1)].rearrange("a p g -> (a p) g")).then_inc(idx_loaded[slot], 16)
                if kind != "plain":
                    if attend:
                        wait(sp, turned[slot], i)
                    else:
                        wait(sp, sum_made[slot], i)
                    if not is_last:
                        sp.dma_start(attr[:, slot, :, :].rearrange("p g f -> p (g f)"),
                                     attr_full[ds(b, 1)].rearrange("a p f -> (a p) f")).then_inc(attr_loaded[slot], 16)
                    else:
                        rest = attr_d[FULL * EPB:E, :]
                        whole, part = REST // COLS, REST % COLS
                        sp.dma_start(attr[0:whole, slot, :, :].rearrange("p g f -> p (g f)"),
                                     rest[0:whole * COLS, :].rearrange("(p g) f -> p (g f)", g=COLS))\
                            .then_inc(attr_loaded[slot], 16)
                        if part:
                            sp.dma_start(attr[whole:whole + 1, slot, 0:part, :].rearrange("p g f -> p (g f)"),
                                         rest[whole * COLS:REST, :].rearrange("(p g) f -> p (g f)", g=part))\
                                .then_inc(attr_loaded[slot], 16)
                if attend:
                    base = sp.value_load(c.base_i[0:1, ds(b, 1)], min_val=0, max_val=N - 1)
                    wait(sp, msg_made[slot], i)
                    sp.dma_start(q_win[:, slot, :], c.q_table[ds(base, WIN), :]).then_inc(q_loaded[slot], 16)

            pairs(sp, loads)

        @block.gpsimd
        def _(pool):
            free = msg_made if attend else sum_made if relu else seg_done

            def gathers(i, slot, is_first, is_last):
                pool.wait_ge(idx_loaded[slot], i * 16 + 16)
                wait(pool, free[slot], i)
                pool.sem_inc(s["begun"], 1)
                for g in range(COLS):
                    pool.indirect_dma_start(got[:, slot, g, :], None, table[:, :],
                                            bass.IndirectOffsetOnAxis(ap=idx[:, slot, g:g + 1], axis=0))\
                        .then_inc(gathered[slot], 16)

            pairs(pool, gathers)

        @block.tensor
        def _(pe):
            def sum_messages(slot, n):
                wait(pe, added[slot], n - 1)
                pe.wait_ge(onehot_made[slot], n)
                if kind == "plain":
                    pe.wait_ge(gathered[slot], have + n * GATHERED)
                else:
                    pe.wait_ge(msg_made[slot], n)
                of = got if kind == "plain" else msg
                for g in range(COLS):
                    ins = pe.matmul(ps_seg[0:rows, slot, 0:WIN], of[:, slot, g, :], onehot[:, slot, g, :],
                                    start=(g == 0), stop=(g == COLS - 1))
                ins.then_inc(seg_done[slot], 1)

            def products(i, slot, is_first, is_last):
                b = 2 * i + slot
                more = 16 if is_last and REST % COLS else 0
                pe.wait_ge(attr_loaded[slot], i * 16 + 16 + more)
                pe.wait_ge(onehot_made[slot], i + 1)
                for j in range(2):
                    wait(pe, s["attr_copied"], b * 2 + j)
                    for k in range(SUB):
                        ins = pe.transpose(ps_at[0:D, k * P:(k + 1) * P], attr[:, slot, j * SUB + k, :], c.ident[:, :])
                    ins.then_inc(s["attr_turned"], 1)
                    wait(pe, s["onehot_copied"], b * 2 + j)
                    pe.sem_inc(s["begun"], 1)
                    for k in range(SUB):
                        ins = pe.transpose(ps_oh[0:WIN, k * P:(k + 1) * P], onehot[:, slot, j * SUB + k, :], c.ident[:, :])
                    ins.then_inc(s["onehot_turned"], 1)
                pe.wait_ge(q_loaded[slot], i * 16 + 16)
                wait(pe, s["eq_used"], b * 2)
                for j in range(2):
                    pe.wait_ge(s["attr_copied"], b * 2 + 1 + j)
                    pe.wait_ge(s["onehot_copied"], b * 2 + 1 + j)
                    for k in range(SUB):
                        pe.matmul(ps_e[:, j, k * D:(k + 1) * D], attr_t[:, j, k * P:(k + 1) * P], c.w_e[:, :],
                                  start=True, stop=True)
                        ins = pe.matmul(ps_q[:, j, k * D:(k + 1) * D], onehot_t[:, j, k * P:(k + 1) * P], q_win[:, slot, :],
                                        start=True, stop=True)
                    ins.then_inc(s["eq_ready"], 1)
                if not is_first:
                    sum_messages(*before(i, slot))

            if attend:
                pe.wait_ge(s["set_up"], 1)
                pairs(pe, products)
                sum_messages(1, PAIRS)
            else:
                pairs(pe, lambda i, slot, is_first, is_last: sum_messages(slot, i + 1))

        @block.scalar
        def _(act):
            def weights(slot, n, b):
                act.wait_ge(s["score_ready"], b)
                wait(act, seg_done[slot], n - 1)
                act.activation(msg[:, slot, :, D:D + H], clipped[:, :, :], ACT.Exp, scale=HD ** -0.5)\
                    .then_inc(s["exp_done"], 1)

            def copies(i, slot, is_first, is_last):
                b = 2 * i + slot
                wait(act, s["eq_ready"], b * 2)
                for j in range(2):
                    act.wait_ge(s["attr_turned"], b * 2 + 1 + j)
                    ins = act.activation(attr_t[0:D, j, :], ps_at[0:D, :], ACT.Copy).then_inc(s["attr_copied"], 1)
                    if j == 1:
                        act.sem_inc(turned[slot], 1)
                    act.wait_ge(s["onehot_turned"], b * 2 + 1 + j)
                    act.activation(onehot_t[:, j, :], ps_oh[0:WIN, :], ACT.Copy).then_inc(s["onehot_copied"], 1)
                if not is_first:
                    weights(*before(i, slot), b)

            def rectify(i, slot, is_first, is_last):
                act.wait_ge(sum_made[slot], i + 1)
                wait(act, seg_done[slot], i)
                act.activation(msg[:, slot, :, :], total[:, slot, :, :], ACT.Relu).then_inc(msg_made[slot], 1)

            if attend:
                pairs(act, copies)
                weights(1, PAIRS, NB)
            if relu:
                pairs(act, rectify)

        @block.vector
        def _(dve):
            def make_onehot(b, slot):
                rel = c.rel[:, ds(b * COLS, COLS)].unsqueeze(2).to_broadcast([P, COLS, WIN])
                dve.tensor_tensor(onehot[:, slot, :, :], c.iota[:, :].unsqueeze(1).to_broadcast([P, COLS, WIN]),
                                  rel, ALU.is_equal).then_inc(onehot_made[slot], 1)

            def add_sums(b, slot, n):
                base = dve.value_load(c.base_i[0:1, ds(b, 1)], min_val=0, max_val=N - 1)
                wait(dve, added[1 - slot], n if slot else n - 1)
                dve.wait_ge(seg_done[slot], n)
                at = c.sums[0:rows, ds(base, WIN)]
                dve.tensor_tensor(at, at, ps_seg[0:rows, slot, 0:WIN], ALU.add).then_inc(added[slot], 1)

            def turn(i, slot, is_first, is_last):
                b = 2 * i + slot
                if attend:
                    ch = Chain(dve, s["chain"], b, 5)
                    dve.wait_ge(gathered[slot], have + i * GATHERED + GATHERED)
                    for j in range(2):
                        of = slice(j * SUB, (j + 1) * SUB)
                        dve.wait_ge(s["eq_ready"], b * 2 + 1 + j)
                        ch.then(dve.tensor_tensor(key_edge[:, of, :], got[:, slot, of, 0:D],
                                                  ps_e[:, j, 0:SUB * D].rearrange("p (k f) -> p k f", f=D), ALU.mult))
                        ch.then(dve.tensor_tensor(prod[:, of, :], key_edge[:, of, :],
                                                  ps_q[:, j, 0:SUB * D].rearrange("p (k f) -> p k f", f=D), ALU.mult))
                        dve.sem_inc(s["eq_used"], 1)
                    ch.then(dve.tensor_reduce(score[:, :, :], prod[:, :, :].rearrange("p g (h d) -> p g h d", d=HD),
                                              AX_X, ALU.add))
                    dve.tensor_scalar(clipped[:, :, :], score[:, :, :], CLIP, -CLIP, ALU.min, ALU.max)\
                        .then_inc(s["score_ready"], 1)
                if relu:
                    more = 16 if is_last and REST % COLS else 0
                    dve.wait_ge(gathered[slot], have + i * GATHERED + GATHERED)
                    dve.wait_ge(attr_loaded[slot], i * 16 + 16 + more)
                    wait(dve, msg_made[slot], i)
                    dve.tensor_tensor(total[:, slot, :, :], got[:, slot, :, :], attr[:, slot, :, :], ALU.add)\
                        .then_inc(sum_made[slot], 1)
                old, n = before(i, slot)
                if not is_first:
                    add_sums(b - 1, old, n)
                if not is_last:
                    make_onehot(b + 1, old)
                if attend:
                    dve.wait_ge(s["exp_done"], b + 1)
                    dve.tensor_tensor(msg[:, slot, :, 0:D].rearrange("p g (h d) -> p g h d", d=HD),
                                      got[:, slot, :, D:2 * D].rearrange("p g (h d) -> p g h d", d=HD),
                                      msg[:, slot, :, D:D + H].unsqueeze(3).to_broadcast([P, COLS, H, HD]),
                                      ALU.mult).then_inc(msg_made[slot], 1)

            if attend:
                ch = Chain(dve, s["set_up"])
                dve.memset(attr_t[D:D + 1, :, :], 1.0)
                dve.memset(msg[:, :, :, MROWS - 1:MROWS], 1.0)
                dve.drain().then_inc(s["set_up"], 1)
            make_onehot(0, 0)
            pairs(dve, turn)
            add_sums(NB - 1, 1, PAIRS)



def layer_norm(dve, ch, c, s, t, n, h, out):
    for k in range(ST):
        ins = dve.bn_stats(n.stats[:, k, :], h[:, k, :])
    ch.then(ins)
    dve.sem_inc(s["taken"], 1)
    for k in range(ST):
        ins = dve.bn_aggr(n.moments[:, k, :], n.stats[:, k, :])
    ins.then_inc(s["var_ready"], 1)
    dve.wait_ge(s["root_ready"], t + 1)
    ch.then(dve.reciprocal(n.rstd[:, :], n.root[:, :]))
    for k in range(ST):
        ins = dve.tensor_scalar(out[:, k, :], h[:, k, :], n.moments[:, k, 0:1], n.rstd[:, k:k + 1],
                                ALU.subtract, ALU.mult)
    return ins


def root_of_var(act, c, s, t, n):
    act.wait_ge(s["var_ready"], t + 1)
    act.activation(n.root[:, :], n.moments[:, :, 1], ACT.Sqrt, bias=c.eps[0:TN, 0:1]).then_inc(s["root_ready"], 1)


class Norm:
    def __init__(self, nc, ctx):
        def sb(name, shape):
            return ctx.enter_context(sbuf(nc, name, shape, F32))

        self.stats = sb("ln_stats", [TN, ST, 6])
        self.moments = sb("ln_moments", [TN, ST, 2])
        self.root = sb("ln_root", [TN, ST])
        self.rstd = sb("ln_rstd", [TN, ST])


def step_rows(table, t):
    return table.rearrange("(t k p) f -> t p k f", k=ST, p=TN)[ds(t, 1)].rearrange("a p k f -> (a p) k f")


def store_steps(sp, s, table, rows):
    def turn(t):
        sp.wait_ge(s["rows_ready"], t + 1)
        sp.dma_start(step_rows(table, t), rows).then_inc(s["stored"], 16)

    steps(sp, turn)
    sp.wait_ge(s["stored"], 16 * STEPS)


def span(t):
    return ds(t * SN, SN)


def psum_tile_at(k):
    return k * TN if k < 4 else 512


def after_attention(nc, c, table):
    with ExitStack() as ctx:
        s = semaphores(nc, ctx, ["sums_copied", "turned", "var_ready", "taken", "root_ready", "rows_ready", "stored", "chain",
                           "kept"], "attention")
        sums_step = ctx.enter_context(sbuf(nc, "sums_step", [MROWS, SN], F32))
        h = ctx.enter_context(sbuf(nc, "h", [TN, ST, D], F32))
        rows = ctx.enter_context(sbuf(nc, "rows", [TN, ST, D], F32))
        z = ctx.enter_context(sbuf(nc, "z", [TN, ST, H], F32))
        zr = ctx.enter_context(sbuf(nc, "zr", [TN, ST, H], F32))
        ps = ctx.enter_context(psum(nc, "ps", [P, 2 * 512], F32))
        psk = ps[0:TN, 0:ST * P].rearrange("p (k f) -> p k f", f=P)
        n = Norm(nc, ctx)
        with nc.Block() as block:
            @block.sync
            def _(sp):
                store_steps(sp, s, table, rows[:, :, :])

            @block.scalar
            def _(act):
                def turn(t):
                    wait(act, s["turned"], t)
                    act.activation(sums_step[:, :], c.sums[0:MROWS, span(t)], ACT.Copy).then_inc(s["sums_copied"], 1)
                    root_of_var(act, c, s, t, n)
                    act.wait_ge(s["rows_ready"], t + 1)
                    act.activation(c.x_nodes[:, ds(t * ST, ST), :], rows[:, :, :], ACT.Copy).then_inc(s["kept"], 1)

                steps(act, turn)

            @block.tensor
            def _(pe):
                def turn(t):
                    pe.wait_ge(s["sums_copied"], t + 1)
                    wait(pe, s["rows_ready"], t)
                    for k in range(ST):
                        ins = pe.transpose(ps[0:TN, k * P:k * P + MROWS], sums_step[:, k * TN:(k + 1) * TN],
                                           c.ident[0:MROWS, 0:MROWS])
                    ins.then_inc(s["turned"], 1)

                steps(pe, turn)

            @block.vector
            def _(dve):
                def turn(t):
                    ch = Chain(dve, s["chain"], t, 7)
                    dve.wait_ge(s["turned"], t + 1)
                    dve.tensor_copy(c.deg[:, ds(t * ST, ST)], psk[:, :, MROWS - 1])
                    ch.then(dve.tensor_scalar(z[:, :, :], psk[:, :, D:D + H], 1e-6, None, ALU.add))
                    ch.then(dve.reciprocal(zr[:, :, :], z[:, :, :]))
                    ch.then(dve.tensor_tensor(h[:, :, :].rearrange("p k (h d) -> p k h d", d=HD),
                                              psk[:, :, 0:D].rearrange("p k (h d) -> p k h d", d=HD),
                                              zr[:, :, :].unsqueeze(3).to_broadcast([TN, ST, H, HD]), ALU.mult))
                    ch.then(dve.tensor_tensor(h[:, :, :], h[:, :, :], c.x_nodes[:, ds(t * ST, ST), :], ALU.add))
                    wait(dve, s["stored"], t * 16)
                    wait(dve, s["kept"], t)
                    ins = layer_norm(dve, ch, c, s, t, n, h, rows)
                    ins.then_inc(s["rows_ready"], 1)
                    ch.then(dve.memset(z[:, :, :], 0.0))

                steps(dve, turn)
        clear_semaphores(nc, s)
        s2 = semaphores(nc, ctx, ["chain", "plus_one", "rooted"], "degree")
        d1 = ctx.enter_context(sbuf(nc, "d1", [TN, TILES], F32))
        d2 = ctx.enter_context(sbuf(nc, "d2", [TN, TILES], F32))
        with nc.Block() as block:
            @block.vector
            def _(dve):
                dve.tensor_scalar(d1[:, :], c.deg[:, :], 1.0, 1.0, ALU.add, ALU.max).then_inc(s2["plus_one"], 1)
                dve.wait_ge(s2["rooted"], 1)
                dve.reciprocal(c.dis[:, :], d2[:, :])

            @block.scalar
            def _(act):
                act.wait_ge(s2["plus_one"], 1)
                act.activation(d2[:, :], d1[:, :], ACT.Sqrt).then_inc(s2["rooted"], 1)
        clear_semaphores(nc, s2)


def clear_sums(nc, c):
    with ExitStack() as ctx:
        s = semaphores(nc, ctx, ["chain"], "clear")
        with nc.Block() as block:
            @block.vector
            def _(dve):
                ch = Chain(dve, s["chain"])
                dve.memset(c.sums[0:D, :], 0.0)
                ch.then(dve.memset(c.round_base[:, :], 0.0))
        clear_semaphores(nc, s)


def after_mean(nc, c, table):
    with ExitStack() as outer:
        ht = outer.enter_context(sbuf(nc, "ht", [D, N], F32))
        stats = outer.enter_context(sbuf(nc, "bn_stats", [D, STEPS * 2, 6], F32))
        with ExitStack() as ctx:
            s = semaphores(nc, ctx, ["x_copied", "counts", "turned", "turned_copied", "mean_ready", "multiplied", "h_ready",
                               "stats_done", "chain"], "mean")
            xs = ctx.enter_context(sbuf(nc, "xs", [TN, ST, D], F32))
            xt = ctx.enter_context(sbuf(nc, "xt", [D, SN], F32))
            inv = ctx.enter_context(sbuf(nc, "inv", [D, SN], F32))
            deg = ctx.enter_context(sbuf(nc, "deg_step", [D, SN], F32))
            mean = ctx.enter_context(sbuf(nc, "mean_step", [D, SN], F32))
            ps_t = ctx.enter_context(psum(nc, "ps_t", [P, 1024], F32))
            ps_d = ctx.enter_context(psum(nc, "ps_d", [P, 1024], F32))
            ps_h = ctx.enter_context(psum(nc, "ps_h", [P, 1024], F32))
            with nc.Block() as block:
                @block.scalar
                def _(act):
                    def turn(t):
                        wait(act, s["turned"], t)
                        act.activation(xs[:, :, :], c.x_nodes[:, ds(t * ST, ST), :], ACT.Copy).then_inc(s["x_copied"], 1)
                        act.wait_ge(s["turned"], t + 1)
                        wait(act, s["multiplied"], t)
                        for i, (a, q, w) in enumerate(PIECES):
                            ins = act.activation(xt[:, a:a + w], ps_t[0:D, q:q + w], ACT.Copy)
                        ins.then_inc(s["turned_copied"], 1)
                        act.wait_ge(s["multiplied"], t + 1)
                        for a, q, w in PIECES:
                            ins = act.activation(ht[:, ds(t * SN + a, w)], ps_h[0:D, q:q + w], ACT.Identity,
                                                 bias=c.b_l[:, 0:1])
                        ins.then_inc(s["h_ready"], 1)

                    steps(act, turn)

                @block.tensor
                def _(pe):
                    def turn(t):
                        wait(pe, s["mean_ready"], t)
                        for a, q, w in PIECES:
                            ins = pe.matmul(ps_d[0:D, q:q + w], c.count_row[0:MROWS, :], c.sums[0:MROWS, ds(t * SN + a, w)],
                                            start=True, stop=True)
                        ins.then_inc(s["counts"], 1)
                        pe.wait_ge(s["x_copied"], t + 1)
                        wait(pe, s["turned_copied"], t)
                        for k in range(ST):
                            q = psum_tile_at(k)
                            ins = pe.transpose(ps_t[0:D, q:q + TN], xs[:, k, :], c.ident[0:TN, 0:TN])
                        ins.then_inc(s["turned"], 1)
                        pe.wait_ge(s["turned_copied"], t + 1)
                        pe.wait_ge(s["mean_ready"], t + 1)
                        wait(pe, s["h_ready"], t)
                        for a, q, w in PIECES:
                            pe.matmul(ps_h[0:D, q:q + w], c.w_l[:, :], mean[:, a:a + w], start=True, stop=False)
                            ins = pe.matmul(ps_h[0:D, q:q + w], c.w_r[:, :], xt[:, a:a + w], start=False, stop=True)
                        ins.then_inc(s["multiplied"], 1)

                    steps(pe, turn)

                @block.vector
                def _(dve):
                    def turn(t):
                        ch = Chain(dve, s["chain"], t, 2)
                        dve.wait_ge(s["counts"], t + 1)
                        for a, q, w in PIECES:
                            ins = dve.tensor_scalar(deg[:, a:a + w], ps_d[0:D, q:q + w], 1.0, None, ALU.max)
                        ch.then(ins)
                        ch.then(dve.reciprocal(inv[:, :], deg[:, :]))
                        wait(dve, s["multiplied"], t)
                        dve.tensor_tensor(mean[:, :], c.sums[0:D, span(t)], inv[:, :], ALU.mult).then_inc(s["mean_ready"], 1)
                        dve.wait_ge(s["h_ready"], t + 1)
                        for i, (a, q, w) in enumerate(PIECES):
                            dve.bn_stats(stats[:, ds(t * 2 + i, 1), :].rearrange("p a b -> p (a b)"),
                                         ht[:, ds(t * SN + a, w)])

                    steps(dve, turn)
            clear_semaphores(nc, s)
        with ExitStack() as ctx:
            s = semaphores(nc, ctx, ["chain", "bn_var", "bn_root", "scaled", "h_ready", "turned", "var_ready", "taken", "root_ready",
                               "rows_ready", "stored", "kept", "normed"], "batch")
            mv = ctx.enter_context(sbuf(nc, "bn_mv", [D, 8], F32))
            hs = ctx.enter_context(sbuf(nc, "hs", [D, SN], F32))
            h = ctx.enter_context(sbuf(nc, "h", [TN, ST, D], F32))
            normed = ctx.enter_context(sbuf(nc, "normed", [TN, ST, D], F32))
            rows = ctx.enter_context(sbuf(nc, "rows", [TN, ST, D], F32))
            ps_n = ctx.enter_context(psum(nc, "ps_n", [P, ST, D], F32))
            n = Norm(nc, ctx)
            with nc.Block() as block:
                @block.sync
                def _(sp):
                    store_steps(sp, s, table, rows[:, :, :])

                @block.scalar
                def _(act):
                    act.wait_ge(s["bn_var"], 1)
                    act.activation(mv[:, 2:3], mv[:, 1:2], ACT.Sqrt, bias=c.eps[0:D, 0:1]).then_inc(s["bn_root"], 1)
                    act.wait_ge(s["scaled"], 1)
                    def turn(t):
                        wait(act, s["turned"], t)
                        act.activation(hs[:, :], ht[:, span(t)], ACT.Relu, bias=mv[:, 6:7], scale=mv[:, 4:5])\
                            .then_inc(s["h_ready"], 1)
                        root_of_var(act, c, s, t, n)
                        act.wait_ge(s["normed"], t + 1)
                        act.activation(c.x_nodes[:, ds(t * ST, ST), :], normed[:, :, :], ACT.Copy).then_inc(s["kept"], 1)

                    steps(act, turn)

                @block.tensor
                def _(pe):
                    def turn(t):
                        pe.wait_ge(s["h_ready"], t + 1)
                        wait(pe, s["normed"], t)
                        for k in range(ST):
                            ins = pe.transpose(ps_n[0:TN, k, :], hs[:, k * TN:(k + 1) * TN], c.ident[0:D, 0:D])
                        ins.then_inc(s["turned"], 1)

                    steps(pe, turn)

                @block.vector
                def _(dve):
                    ch = Chain(dve, s["bn_var"])
                    ch.then(dve.bn_aggr(mv[:, 0:2], stats[:, :, :].rearrange("p a b -> p (a b)")))
                    dve.wait_ge(s["bn_root"], 1)
                    ch.then(dve.reciprocal(mv[:, 3:4], mv[:, 2:3]))
                    ch.then(dve.tensor_tensor(mv[:, 4:5], mv[:, 3:4], c.gamma[:, :], ALU.mult))
                    ch.then(dve.tensor_tensor(mv[:, 5:6], mv[:, 0:1], mv[:, 4:5], ALU.mult))
                    dve.tensor_tensor(mv[:, 6:7], c.beta[:, :], mv[:, 5:6], ALU.subtract).then_inc(s["scaled"], 1)
                    def turn(t):
                        ch = Chain(dve, s["chain"], t, 3)
                        dve.wait_ge(s["turned"], t + 1)
                        ch.then(dve.tensor_tensor(h[:, :, :], ps_n[0:TN, :, :], c.x_nodes[:, ds(t * ST, ST), :], ALU.add))
                        wait(dve, s["kept"], t)
                        layer_norm(dve, ch, c, s, t, n, h, normed).then_inc(s["normed"], 1)
                        dve.wait_ge(s["normed"], t + 1)
                        wait(dve, s["stored"], t * 16)
                        dve.tensor_tensor(rows[:, :, :], normed[:, :, :],
                                          c.dis[:, ds(t * ST, ST)].unsqueeze(2).to_broadcast([TN, ST, D]), ALU.mult)\
                            .then_inc(s["rows_ready"], 1)

                    steps(dve, turn)
            clear_semaphores(nc, s)


def after_first_convolution(nc, c, table):
    with ExitStack() as ctx:
        s = semaphores(nc, ctx, ["y_made", "turned", "counts", "plus_one", "rooted", "s_ready", "local_done", "local_kept",
                           "g_done", "g_ready", "y_ready", "y_turned", "rows_ready", "stored", "chain"], "conv")
        ys = ctx.enter_context(sbuf(nc, "ys", [TN, ST, D], F32))
        deg = ctx.enter_context(sbuf(nc, "deg_step", [D, SN], F32))
        root = ctx.enter_context(sbuf(nc, "root_step", [D, SN], F32))
        dis = ctx.enter_context(sbuf(nc, "dis_step", [D, SN], F32))
        nb = ctx.enter_context(sbuf(nc, "nb_step", [D, SN], F32))
        g = ctx.enter_context(sbuf(nc, "g_step", [D, SN], F32))
        yt = ctx.enter_context(sbuf(nc, "yt_step", [D, SN], F32))
        rows = ctx.enter_context(sbuf(nc, "rows", [TN, ST, D], F32))
        ps_t = ctx.enter_context(psum(nc, "ps_t", [P, 1024], F32))
        ps_d = ctx.enter_context(psum(nc, "ps_d", [P, 1024], F32))
        ps_l = ctx.enter_context(psum(nc, "ps_l", [P, 1024], F32))
        ps_n = ctx.enter_context(psum(nc, "ps_n", [P, ST, D], F32))
        with nc.Block() as block:
            @block.sync
            def _(sp):
                store_steps(sp, s, table, rows[:, :, :])

            @block.tensor
            def _(pe):
                def turn(t):
                    wait(pe, s["plus_one"], t)
                    for a, q, w in PIECES:
                        ins = pe.matmul(ps_d[0:D, q:q + w], c.count_row[0:MROWS, :], c.sums[0:MROWS, ds(t * SN + a, w)],
                                        start=True, stop=True)
                    ins.then_inc(s["counts"], 1)
                    pe.wait_ge(s["y_made"], t + 1)
                    wait(pe, s["g_ready"], t)
                    for k in range(ST):
                        q = psum_tile_at(k)
                        ins = pe.transpose(ps_t[0:D, q:q + TN], ys[:, k, :], c.ident[0:TN, 0:TN])
                    ins.then_inc(s["turned"], 1)
                    pe.wait_ge(s["s_ready"], t + 1)
                    wait(pe, s["local_kept"], t)
                    for a, q, w in PIECES:
                        ins = pe.matmul(ps_l[0:D, q:q + w], c.w_local[:, :], nb[:, a:a + w], start=True, stop=True)
                    ins.then_inc(s["local_done"], 1)
                    for a, q, w in PIECES:
                        ins = pe.matmul(ps_t[0:D, q:q + w], c.w_g1[:, :], nb[:, a:a + w], start=True, stop=True)
                    ins.then_inc(s["g_done"], 1)
                    pe.wait_ge(s["y_ready"], t + 1)
                    wait(pe, s["rows_ready"], t)
                    for k in range(ST):
                        ins = pe.transpose(ps_n[0:TN, k, :], yt[:, k * TN:(k + 1) * TN], c.ident[0:D, 0:D])
                    ins.then_inc(s["y_turned"], 1)

                steps(pe, turn)

            @block.scalar
            def _(act):
                def turn(t):
                    act.wait_ge(s["plus_one"], t + 1)
                    act.activation(root[:, :], deg[:, :], ACT.Sqrt).then_inc(s["rooted"], 1)
                    act.wait_ge(s["local_done"], t + 1)
                    for a, q, w in PIECES:
                        ins = act.activation(c.local_t[:, ds(t * SN + a, w)], ps_l[0:D, q:q + w], ACT.Relu,
                                             bias=c.b_local[:, 0:1])
                    ins.then_inc(s["local_kept"], 1)
                    act.wait_ge(s["g_done"], t + 1)
                    for a, q, w in PIECES:
                        ins = act.activation(g[:, a:a + w], ps_t[0:D, q:q + w], ACT.Relu, bias=c.b_g1[:, 0:1])
                    ins.then_inc(s["g_ready"], 1)
                    act.wait_ge(s["y_turned"], t + 1)
                    wait(act, s["stored"], t * 16)
                    act.activation(rows[:, :, :], ps_n[0:TN, :, :], ACT.Copy).then_inc(s["rows_ready"], 1)

                steps(act, turn)

            @block.vector
            def _(dve):
                def turn(t):
                    ch = Chain(dve, s["chain"], t, 4)
                    wait(dve, s["turned"], t)
                    dve.tensor_tensor(ys[:, :, :], c.x_nodes[:, ds(t * ST, ST), :],
                                      c.dis[:, ds(t * ST, ST)].unsqueeze(2).to_broadcast([TN, ST, D]), ALU.mult)\
                        .then_inc(s["y_made"], 1)
                    dve.wait_ge(s["counts"], t + 1)
                    wait(dve, s["rooted"], t)
                    for a, q, w in PIECES:
                        ins = dve.tensor_scalar(deg[:, a:a + w], ps_d[0:D, q:q + w], 1.0, 1.0, ALU.add, ALU.max)
                    ins.then_inc(s["plus_one"], 1)
                    dve.wait_ge(s["rooted"], t + 1)
                    ch.then(dve.reciprocal(dis[:, :], root[:, :]))
                    dve.wait_ge(s["turned"], t + 1)
                    wait(dve, s["g_done"], t)
                    for a, q, w in PIECES:
                        ins = dve.tensor_tensor(nb[:, a:a + w], c.sums[0:D, ds(t * SN + a, w)], ps_t[0:D, q:q + w], ALU.add)
                    ch.then(ins)
                    dve.tensor_tensor(nb[:, :], nb[:, :], dis[:, :], ALU.mult).then_inc(s["s_ready"], 1)
                    dve.wait_ge(s["g_ready"], t + 1)
                    wait(dve, s["y_turned"], t)
                    ch.then(dve.tensor_tensor(yt[:, :], g[:, :], dis[:, :], ALU.mult))
                    dve.sem_inc(s["y_ready"], 1)
                    ch.then(dve.tensor_copy(c.y_t[:, span(t)], yt[:, :]))

                steps(dve, turn)
        clear_semaphores(nc, s)


def after_second_convolution(nc, c, table):
    with ExitStack() as ctx:
        s = semaphores(nc, ctx, ["counts", "plus_one", "rooted", "s_ready", "g_done", "g_ready", "local_ready", "fused",
                           "var_ready", "taken", "root_ready", "rows_ready", "stored", "kept", "chain", "ones_made"], "fuse")
        deg = ctx.enter_context(sbuf(nc, "deg_step", [D, SN], F32))
        root = ctx.enter_context(sbuf(nc, "root_step", [D, SN], F32))
        dis = ctx.enter_context(sbuf(nc, "dis_step", [D, SN], F32))
        nb = ctx.enter_context(sbuf(nc, "nb_step", [D, SN], F32))
        g = ctx.enter_context(sbuf(nc, "g_step", [D, SN], F32))
        local = ctx.enter_context(sbuf(nc, "local_step", [D + 1, SN], F32))
        h = ctx.enter_context(sbuf(nc, "h", [TN, ST, D], F32))
        rows = ctx.enter_context(sbuf(nc, "rows", [TN, ST, D], F32))
        ps_d = ctx.enter_context(psum(nc, "ps_d", [P, 1024], F32))
        ps_g = ctx.enter_context(psum(nc, "ps_g", [P, 1024], F32))
        ps_n = ctx.enter_context(psum(nc, "ps_n", [P, ST, D], F32))
        n = Norm(nc, ctx)
        with nc.Block() as block:
            @block.sync
            def _(sp):
                store_steps(sp, s, table, rows[:, :, :])

            @block.tensor
            def _(pe):
                def turn(t):
                    wait(pe, s["plus_one"], t)
                    for a, q, w in PIECES:
                        ins = pe.matmul(ps_d[0:D, q:q + w], c.count_row[0:MROWS, :], c.sums[0:MROWS, ds(t * SN + a, w)],
                                        start=True, stop=True)
                    ins.then_inc(s["counts"], 1)
                    pe.wait_ge(s["s_ready"], t + 1)
                    wait(pe, s["g_ready"], t)
                    for a, q, w in PIECES:
                        ins = pe.matmul(ps_g[0:D, q:q + w], c.w_g2[:, :], nb[:, a:a + w], start=True, stop=True)
                    ins.then_inc(s["g_done"], 1)
                    pe.wait_ge(s["g_ready"], t + 1)
                    pe.wait_ge(s["local_ready"], t + 1)
                    pe.wait_ge(s["ones_made"], 1)
                    wait(pe, s["rows_ready"], t)
                    for k in range(ST):
                        at = slice(k * TN, (k + 1) * TN)
                        pe.matmul(ps_n[0:TN, k, :], local[:, at], c.w_f1[:, :], start=True, stop=False)
                        ins = pe.matmul(ps_n[0:TN, k, :], g[:, at], c.w_f2[:, :], start=False, stop=True)
                    ins.then_inc(s["fused"], 1)

                steps(pe, turn)

            @block.scalar
            def _(act):
                def turn(t):
                    wait(act, s["fused"], t)
                    act.activation(local[0:D, :], c.local_t[:, span(t)], ACT.Copy).then_inc(s["local_ready"], 1)
                    act.wait_ge(s["plus_one"], t + 1)
                    act.activation(root[:, :], deg[:, :], ACT.Sqrt).then_inc(s["rooted"], 1)
                    act.wait_ge(s["g_done"], t + 1)
                    for a, q, w in PIECES:
                        ins = act.activation(g[:, a:a + w], ps_g[0:D, q:q + w], ACT.Relu, bias=c.b_g2[:, 0:1])
                    ins.then_inc(s["g_ready"], 1)
                    root_of_var(act, c, s, t, n)
                    act.wait_ge(s["rows_ready"], t + 1)
                    act.activation(c.x_nodes[:, ds(t * ST, ST), :], rows[:, :, :], ACT.Copy).then_inc(s["kept"], 1)

                steps(act, turn)

            @block.vector
            def _(dve):
                dve.memset(local[D:D + 1, :], 1.0).then_inc(s["ones_made"], 1)
                def turn(t):
                    ch = Chain(dve, s["chain"], t, 5)
                    dve.wait_ge(s["counts"], t + 1)
                    for a, q, w in PIECES:
                        ins = dve.tensor_scalar(deg[:, a:a + w], ps_d[0:D, q:q + w], 1.0, 1.0, ALU.add, ALU.max)
                    ins.then_inc(s["plus_one"], 1)
                    dve.wait_ge(s["rooted"], t + 1)
                    ch.then(dve.reciprocal(dis[:, :], root[:, :]))
                    wait(dve, s["g_done"], t)
                    ch.then(dve.tensor_tensor(nb[:, :], c.sums[0:D, span(t)], c.y_t[:, span(t)], ALU.add))
                    dve.tensor_tensor(nb[:, :], nb[:, :], dis[:, :], ALU.mult).then_inc(s["s_ready"], 1)
                    dve.wait_ge(s["fused"], t + 1)
                    ch.then(dve.tensor_tensor(h[:, :, :], ps_n[0:TN, :, :], c.x_nodes[:, ds(t * ST, ST), :], ALU.add))
                    wait(dve, s["stored"], t * 16)
                    wait(dve, s["kept"], t)
                    layer_norm(dve, ch, c, s, t, n, h, rows).then_inc(s["rows_ready"], 1)

                steps(dve, turn)
        clear_semaphores(nc, s)


def after_edges(nc, c, out):
    with ExitStack() as ctx:
        s = semaphores(nc, ctx, ["x_copied", "turned", "s_ready", "h_done", "h_ready", "out_done", "var_ready", "taken", "root_ready",
                           "rows_ready", "stored", "chain", "ones_made"], "mlp")
        xs = ctx.enter_context(sbuf(nc, "xs", [TN, ST, D], F32))
        st = ctx.enter_context(sbuf(nc, "st", [D, SN], F32))
        hid = ctx.enter_context(sbuf(nc, "hid", [D + 1, SN], F32))
        h = ctx.enter_context(sbuf(nc, "h", [TN, ST, D], F32))
        rows = ctx.enter_context(sbuf(nc, "rows", [TN, ST, D], F32))
        ps_t = ctx.enter_context(psum(nc, "ps_t", [P, 1024], F32))
        ps_h = ctx.enter_context(psum(nc, "ps_h", [P, 1024], F32))
        ps_n = ctx.enter_context(psum(nc, "ps_n", [P, ST, D], F32))
        n = Norm(nc, ctx)
        with nc.Block() as block:
            @block.sync
            def _(sp):
                store_steps(sp, s, out, rows[:, :, :])

            @block.tensor
            def _(pe):
                def turn(t):
                    pe.wait_ge(s["x_copied"], t + 1)
                    wait(pe, s["s_ready"], t)
                    for k in range(ST):
                        q = psum_tile_at(k)
                        ins = pe.transpose(ps_t[0:D, q:q + TN], xs[:, k, :], c.ident[0:TN, 0:TN])
                    ins.then_inc(s["turned"], 1)
                    pe.wait_ge(s["s_ready"], t + 1)
                    wait(pe, s["h_ready"], t)
                    for a, q, w in PIECES:
                        ins = pe.matmul(ps_h[0:D, q:q + w], c.w_1[:, :], st[:, a:a + w], start=True, stop=True)
                    ins.then_inc(s["h_done"], 1)
                    pe.wait_ge(s["h_ready"], t + 1)
                    pe.wait_ge(s["ones_made"], 1)
                    wait(pe, s["rows_ready"], t)
                    for k in range(ST):
                        ins = pe.matmul(ps_n[0:TN, k, :], hid[:, k * TN:(k + 1) * TN], c.w_2[:, :], start=True, stop=True)
                    ins.then_inc(s["out_done"], 1)

                steps(pe, turn)

            @block.scalar
            def _(act):
                def turn(t):
                    wait(act, s["rows_ready"], t)
                    act.activation(xs[:, :, :], c.x_nodes[:, ds(t * ST, ST), :], ACT.Copy).then_inc(s["x_copied"], 1)
                    act.wait_ge(s["h_done"], t + 1)
                    for a, q, w in PIECES:
                        ins = act.activation(hid[0:D, a:a + w], ps_h[0:D, q:q + w], ACT.Relu, bias=c.b_1[:, 0:1])
                    ins.then_inc(s["h_ready"], 1)
                    root_of_var(act, c, s, t, n)

                steps(act, turn)

            @block.vector
            def _(dve):
                dve.memset(hid[D:D + 1, :], 1.0).then_inc(s["ones_made"], 1)
                def turn(t):
                    ch = Chain(dve, s["chain"], t, 4)
                    dve.wait_ge(s["turned"], t + 1)
                    wait(dve, s["h_done"], t)
                    for a, q, w in PIECES:
                        ins = dve.tensor_tensor(st[:, a:a + w], c.sums[0:D, ds(t * SN + a, w)], ps_t[0:D, q:q + w], ALU.add)
                    ins.then_inc(s["s_ready"], 1)
                    dve.wait_ge(s["out_done"], t + 1)
                    ch.then(dve.scalar_tensor_tensor(out=h[:, :, :], in0=ps_n[0:TN, :, :], scalar=0.0, in1=xs[:, :, :],
                                                     op0=ALU.max, op1=ALU.add))
                    ch.then(dve.tensor_tensor(h[:, :, :], h[:, :, :], xs[:, :, :], ALU.add))
                    wait(dve, s["stored"], t * 16)
                    layer_norm(dve, ch, c, s, t, n, h, rows).then_inc(s["rows_ready"], 1)

                steps(dve, turn)
        clear_semaphores(nc, s)


class Chip:

    def __init__(self, nc, ctx):
        def sb(name, shape, dt=F32):
            return ctx.enter_context(sbuf(nc, name, shape, dt))

        self.x_nodes = sb("x_nodes", [TN, TILES, D])
        self.sums = sb("sums", [P, NPAD])
        self.local_t = sb("local_t", [D, N])
        self.y_t = sb("y_t", [D, N])
        self.dst_f = sb("dst_f", [P, NB * COLS])
        self.rel = sb("rel", [P, (NB + 1) * COLS])
        self.first_dst = sb("first_dst", [P, NB])
        self.base_f = sb("base_f", [P, NB])
        self.base_i = sb("base_i", [P, NB], I32)
        self.round_base = sb("round_base", [P, 1])
        self.sorted_ = sb("all_inside", [P, 1])
        self.n_rounds = sb("n_rounds", [P, 1], I32)
        self.eps = sb("eps", [P, 1])
        self.deg = sb("deg", [TN, TILES])
        self.dis = sb("dis", [TN, TILES])
        self.iota = sb("iota", [P, WIN])
        self.ident = sb("ident", [P, P])
        self.count_row = sb("count_row", [P, D])
        self.w_kvq = sb("w_kvq", [D + 1, 3, D])
        self.w_e = sb("w_e", [D + 1, D])
        self.w_f1 = sb("w_f1", [D + 1, D])
        self.w_2 = sb("w_2", [D + 1, D])
        self.w_l = sb("w_l", [D, D])
        self.w_r = sb("w_r", [D, D])
        self.w_local = sb("w_local", [D, D])
        self.w_g1 = sb("w_g1", [D, D])
        self.w_g2 = sb("w_g2", [D, D])
        self.w_f2 = sb("w_f2", [D, D])
        self.w_1 = sb("w_1", [D, D])
        self.b_l = sb("b_l", [D, 1])
        self.gamma = sb("gamma", [D, 1])
        self.beta = sb("beta", [D, 1])
        self.b_local = sb("b_local", [D, 1])
        self.b_g1 = sb("b_g1", [D, 1])
        self.b_g2 = sb("b_g2", [D, 1])
        self.b_1 = sb("b_1", [D, 1])
        self.kv_table = nc.dram_tensor("kv_table", [N, 2 * D], F32).ap()
        self.q_table = nc.dram_tensor("q_table", [NPAD, D], F32).ap()
        self.tables = [nc.dram_tensor(f"node_table{i}", [N, D], F32).ap() for i in range(4)]


def graph_layers(nc, A, out):
    with ExitStack() as ctx:
        c = Chip(nc, ctx)
        gathered = [[ctx.enter_context(nc.semaphore(f"gathered{p}_{s}")) for s in range(2)] for p in range(5)]
        setup(nc, c, A)
        project(nc, c, A)
        rounds = nc.values_load(c.n_rounds[0:1, 0:1], min_val=1, max_val=ROUNDS)

        def edges(n, kind, table):
            with nc.Fori(0, rounds) as r:
                place_windows(nc, c)
                edge_pass(nc, c, A, kind, table, gathered[n], r)

        edges(0, "attend", c.kv_table)
        after_attention(nc, c, c.tables[0])
        clear_sums(nc, c)
        edges(1, "plain", c.tables[0])
        after_mean(nc, c, c.tables[1])
        clear_sums(nc, c)
        edges(2, "plain", c.tables[1])
        after_first_convolution(nc, c, c.tables[2])
        clear_sums(nc, c)
        edges(3, "plain", c.tables[2])
        after_second_convolution(nc, c, c.tables[3])
        clear_sums(nc, c)
        edges(4, "relu", c.tables[3])
        after_edges(nc, c, out)


ROWS = ("L0_gnn_bk", "L0_gnn_bv", "L0_gnn_bq", "L0_gnn_be", "L2_gnn_b_fuse", "L3_gnn_b2")
COLUMNS = ("L1_gnn_bl", "L1_gnn_gamma", "L1_gnn_beta", "L2_gnn_b_local", "L2_gnn_b_g1", "L2_gnn_b_g2", "L3_gnn_b1")


def kernel(**inputs):
    import numpy as np
    import concourse.bacc as bacc
    from concourse.bass_utils import run_bass_kernel_spmd

    arrays = {k: np.asarray(v) for k, v in inputs.items()}
    for k in ROWS:
        arrays[k] = arrays[k].reshape(1, D)
    for k in COLUMNS:
        arrays[k] = arrays[k].reshape(D, 1)
    for k in ("L1_gnn_Wl", "L1_gnn_Wr"):
        arrays[k + "T"] = arrays.pop(k).T
    for k, fill in (("src", 0), ("dst", -1)):
        padded = np.full(NB * EPB, fill, arrays[k].dtype)
        padded[:E] = arrays[k]
        arrays[k] = padded.reshape(NB, P, COLS)
    nc = bacc.Bacc("TRN2", target_bir_lowering=False, num_devices=1)
    aps = {}
    for k in arrays:
        arrays[k] = np.ascontiguousarray(arrays[k])
        aps[k] = nc.dram_tensor(k + "_in", arrays[k].shape, mybir.dt.from_np(arrays[k].dtype), kind="ExternalInput").ap()
    out = nc.dram_tensor("x_out", (N, D), F32, kind="ExternalOutput").ap()
    graph_layers(nc, aps, out)
    r = run_bass_kernel_spmd(nc, [{k + "_in": v for k, v in arrays.items()}], core_ids=[0])
    return r.results[0]["x_out"]
```

```python
from contextlib import ExitStack

import concourse.bass as bass
from concourse import mybir

ALU = mybir.AluOpType
ACT = mybir.ActivationFunctionType
AX_X = mybir.AxisListType.X
F32 = mybir.dt.float32
I32 = mybir.dt.int32
BF16 = mybir.dt.bfloat16
F16 = mybir.dt.float16
F8 = mybir.dt.float8e4
U8 = mybir.dt.uint8
ds = bass.ds

P = 128
N = 6250
D = 96
E = 206250
H = 8
HD = D // H
COLS = 8
EPB = P * COLS
NB = -(-E // EPB)
NB += NB % 2
PAIRS = NB // 2
FULL = E // EPB
REST = E - FULL * EPB
WIN = 48
ROUNDS = -(-N // WIN)
SUB = COLS // 2
MROWS = D + H + 1
PAIR = 2 * 5
GROUP = PAIR // 2
GCOLS = 2
BANKS = 5
SLOTS = 2 * BANKS
GCAP = P * GCOLS
CHUNK = 50 * PAIR
CHUNKS = -(-N // CHUNK)
assert CHUNKS % 2 == 1 and CHUNKS >= 5
GROUPS = CHUNKS * CHUNK // GROUP
NPAD = max(N + WIN, CHUNKS * CHUNK)
EXACT = 16
TN = 125
DTILES = CHUNK // TN
TILES = N // TN
ST = 5
STEPS = TILES // ST
HALF = TILES // 2
SN = ST * TN
CUT = 4 * TN
PIECES = ((0, 0, CUT), (CUT, 512, SN - CUT))
GATHERED = 16 * COLS
EPS = 1e-5
CLIP = 5.0 * HD ** 0.5


def semaphores(nc, ctx, names, tag):
    return {n: ctx.enter_context(nc.semaphore(f"{tag}_{n}")) for n in names}


def clear_semaphores(nc, s):
    with nc.Block() as block:
        @block.vector
        def _(dve):
            for sem in s.values():
                dve.sem_clear(sem)


def clear_gather_semaphores(nc, s):
    with nc.Block() as block:
        @block.gpsimd
        def _(pool):
            pool.dma_reset()
            for sem in s.values():
                pool.sem_clear(sem)


def sbuf(nc, name, shape, dt):
    return nc.sbuf_tensor(f"{name}_{nc.next_id()}", shape, dt)


def psum(nc, name, shape, dt):
    return nc.psum_tensor(f"{name}_{nc.next_id()}", shape, dt)


def wait(eng, sem, count):
    if not (isinstance(count, int) and count == 0):
        eng.wait_ge(sem, count)


def steps(eng, turn):
    turn(0)
    with eng.Fori(1, STEPS) as t:
        turn(t)


class Chain:

    def __init__(self, eng, sem, turn=0, per=0):
        self.eng, self.sem, self.turn, self.per, self.n = eng, sem, turn, per, 0

    def then(self, ins):
        ins.then_inc(self.sem, 1)
        self.n += 1
        self.eng.wait_ge(self.sem, self.turn * self.per + self.n)


def setup(nc, c, A):
    with ExitStack() as ctx:
        s = semaphores(nc, ctx, ["loaded", "made", "chain", "iota_made", "counted", "bases", "summed", "padded"], "setup")
        iota_i = ctx.enter_context(sbuf(nc, "iota_i", [P, WIN], I32))
        dst_i = ctx.enter_context(sbuf(nc, "dst_i", [P, NB * COLS], I32))
        inside = ctx.enter_context(sbuf(nc, "inside", [P, NB * COLS], F32))
        first_row = ctx.enter_context(sbuf(nc, "first_row", [P, P], F32))
        ones = ctx.enter_context(sbuf(nc, "ones", [P, P], F32))
        count = ctx.enter_context(sbuf(nc, "count", [P, 4], F32))
        zero = ctx.enter_context(sbuf(nc, "zero", [WIN, D], F32))
        ps = ctx.enter_context(psum(nc, "setup_ps", [P, 512], F32))
        with nc.Block() as block:
            @block.sync
            def _(sp):
                loads = [
                    (dst_i[:, :], A["dst"].rearrange("b p g -> p b g")),
                    (c.x_nodes[:, :, :], A["x"].rearrange("(t p) f -> p t f", p=TN)),
                    (c.w_kvq[0:D, 0, :], A["L0_gnn_Wk"]), (c.w_kvq[D:D + 1, 0, :], A["L0_gnn_bk"]),
                    (c.w_kvq[0:D, 1, :], A["L0_gnn_Wv"]), (c.w_kvq[D:D + 1, 1, :], A["L0_gnn_bv"]),
                    (c.w_kvq[0:D, 2, :], A["L0_gnn_Wq"]), (c.w_kvq[D:D + 1, 2, :], A["L0_gnn_bq"]),
                    (c.w_e[0:D, :], A["L0_gnn_We"]), (c.w_e[D:D + 1, :], A["L0_gnn_be"]),
                    (c.w_l[:, :], A["L1_gnn_WlT"]), (c.w_r[:, :], A["L1_gnn_WrT"]),
                    (c.w_local[:, :], A["L2_gnn_W_local"]), (c.w_g1[:, :], A["L2_gnn_W_g1"]),
                    (c.w_g2[:, :], A["L2_gnn_W_g2"]),
                    (c.w_f1[0:D, :], A["L2_gnn_W_fuse"][0:D, :]), (c.w_f1[D:D + 1, :], A["L2_gnn_b_fuse"]),
                    (c.w_f2[:, :], A["L2_gnn_W_fuse"][D:2 * D, :]),
                    (c.w_1[:, :], A["L3_gnn_W1"]),
                    (c.w_2[0:D, :], A["L3_gnn_W2"]), (c.w_2[D:D + 1, :], A["L3_gnn_b2"]),
                    (c.b_l[:, :], A["L1_gnn_bl"]), (c.gamma[:, :], A["L1_gnn_gamma"]),
                    (c.beta[:, :], A["L1_gnn_beta"]), (c.b_local[:, :], A["L2_gnn_b_local"]),
                    (c.b_g1[:, :], A["L2_gnn_b_g1"]), (c.b_g2[:, :], A["L2_gnn_b_g2"]),
                    (c.b_1[:, :], A["L3_gnn_b1"]),
                ]
                for to, of in loads:
                    sp.dma_start(to, of).then_inc(s["loaded"], 16)
                sp.wait_ge(s["loaded"], 16 * len(loads))
                sp.sem_inc(s["counted"], 1)
                sp.wait_ge(s["padded"], 1)
                sp.dma_start(c.q_table[N:N + WIN, :], zero[:, :]).then_inc(s["loaded"], 16)
                sp.wait_ge(s["loaded"], 16 * len(loads) + 16)

            @block.gpsimd
            def _(pool):
                pool.iota(iota_i[:, :], pattern=[[1, WIN]], base=0, channel_multiplier=0).then_inc(s["iota_made"], 1)
                pool.memset(c.ident[:, :], 0.0).then_inc(s["made"], 1)
                pool.memset(first_row[:, :], 1.0).then_inc(s["made"], 1)
                pool.memset(c.count_row[:, :], 1.0).then_inc(s["made"], 1)
                pool.wait_ge(s["made"], 3)
                pool.affine_select(out=c.ident[:, :], in_=c.ident[:, :], compare_op=ALU.not_equal, fill=1.0,
                                   base=0, pattern=[[-1, P]], channel_multiplier=1).then_inc(s["made"], 1)
                pool.affine_select(out=first_row[:, :], in_=first_row[:, :], compare_op=ALU.is_equal, fill=0.0,
                                   base=0, pattern=[[0, P]], channel_multiplier=1).then_inc(s["made"], 1)
                pool.affine_select(out=c.count_row[:, :], in_=c.count_row[:, :], compare_op=ALU.is_equal, fill=0.0,
                                   base=-(MROWS - 1), pattern=[[0, D]], channel_multiplier=1).then_inc(s["made"], 1)

            @block.vector
            def _(dve):
                dve.memset(zero[:, :], 0.0).then_inc(s["padded"], 1)
                dve.memset(ones[:, :], 1.0)
                dve.memset(c.sums[:, :], 0.0)
                dve.memset(c.eps[:, :], EPS)
                dve.memset(c.rel[:, NB * COLS:], -1.0)
                ch = Chain(dve, s["chain"])
                ch.then(dve.memset(c.round_base[:, :], 0.0))
                dve.wait_ge(s["iota_made"], 1)
                ch.then(dve.tensor_copy(c.iota[:, :], iota_i[:, :]))
                dve.wait_ge(s["counted"], 1)
                dve.tensor_copy(c.dst_f[:, :], dst_i[:, :]).then_inc(s["bases"], 1)
                dve.wait_ge(s["summed"], 1)
                ch.then(dve.tensor_copy(c.first_dst[:, :], ps[:, 0:NB]))
                rel = c.rel[:, 0:NB * COLS].rearrange("p (b g) -> p b g", g=COLS)
                ch.then(dve.tensor_tensor(rel, c.dst_f[:, :].rearrange("p (b g) -> p b g", g=COLS),
                                          c.first_dst[:, :].unsqueeze(2).to_broadcast([P, NB, COLS]), ALU.subtract))
                ch.then(dve.tensor_scalar(inside[:, :], c.rel[:, 0:NB * COLS], 0.0, None, ALU.is_ge))
                ch.then(dve.scalar_tensor_tensor(out=inside[:, :], in0=c.rel[:, 0:NB * COLS], scalar=float(WIN),
                                                 in1=inside[:, :], op0=ALU.is_lt, op1=ALU.mult))
                dve.tensor_reduce(count[:, 0:1], inside[:, :], AX_X, ALU.add).then_inc(s["bases"], 1)
                dve.wait_ge(s["summed"], 2)
                ch.then(dve.tensor_scalar(c.sorted_[:, :], ps[:, 256:257], float(E), None, ALU.is_equal))
                ch.then(dve.tensor_scalar(count[:, 1:2], c.sorted_[:, :], float(1 - ROUNDS), float(ROUNDS), ALU.mult, ALU.add))
                ch.then(dve.tensor_copy(c.n_rounds[:, :], count[:, 1:2]))

            @block.tensor
            def _(pe):
                pe.wait_ge(s["made"], 6)
                pe.wait_ge(s["bases"], 1)
                pe.matmul(ps[:, 0:NB], first_row[:, :], c.dst_f[:, :].rearrange("p (b g) -> p b g", g=COLS)[:, :, 0],
                          start=True, stop=True).then_inc(s["summed"], 1)
                pe.wait_ge(s["bases"], 2)
                pe.matmul(ps[:, 256:257], ones[:, :], count[:, 0:1], start=True, stop=True).then_inc(s["summed"], 1)
        clear_semaphores(nc, s)


def project(nc, c, A):
    with ExitStack() as ctx:
        s = semaphores(nc, ctx, ["x_loaded", "turned", "turned_copied", "multiplied", "kv_copied", "q_copied", "stored",
                           "ones_made"], "project")
        x_step = ctx.enter_context(sbuf(nc, "x_step", [TN, ST, D], F32))
        xt = ctx.enter_context(sbuf(nc, "xt", [D + 1, SN], F32))
        rows = ctx.enter_context(sbuf(nc, "rows", [TN, ST, 3 * D], F32))
        ps_t = ctx.enter_context(psum(nc, "ps_t", [P, 1024], F32))
        ps_r = ctx.enter_context(psum(nc, "ps_r", [P, ST, 512], F32))
        w = c.w_kvq[:, :, :].rearrange("k a f -> k (a f)")
        with nc.Block() as block:
            @block.sync
            def _(sp):
                def turn(t):
                    wait(sp, s["turned"], t)
                    sp.dma_start(x_step[:, :, :], A["x"].rearrange("(t k p) f -> t p k f", k=ST, p=TN)[ds(t, 1)]
                                 .rearrange("a p k f -> (a p) k f")).then_inc(s["x_loaded"], 16)
                    sp.wait_ge(s["kv_copied"], t + 1)
                    sp.dma_start(c.kv_table.rearrange("(t k p) f -> t p k f", k=ST, p=TN)[ds(t, 1)]
                                 .rearrange("a p k f -> (a p) k f"), rows[:, :, 0:2 * D]).then_inc(s["stored"], 16)
                    sp.wait_ge(s["q_copied"], t + 1)
                    sp.dma_start(c.q_table[0:N, :].rearrange("(t k p) f -> t p k f", k=ST, p=TN)[ds(t, 1)]
                                 .rearrange("a p k f -> (a p) k f"), rows[:, :, 2 * D:]).then_inc(s["stored"], 16)

                steps(sp, turn)
                sp.wait_ge(s["stored"], 32 * STEPS)

            @block.tensor
            def _(pe):
                pe.wait_ge(s["ones_made"], 1)
                def turn(t):
                    pe.wait_ge(s["x_loaded"], t * 16 + 16)
                    for k in range(ST):
                        at = k * TN if k < 4 else 512
                        ins = pe.transpose(ps_t[0:D, at:at + TN], x_step[:, k, :], c.ident[0:TN, 0:TN])
                    ins.then_inc(s["turned"], 1)
                    pe.wait_ge(s["turned_copied"], t + 1)
                    wait(pe, s["kv_copied"], t)
                    wait(pe, s["q_copied"], t)
                    for k in range(ST):
                        ins = pe.matmul(ps_r[0:TN, k, 0:3 * D], xt[:, k * TN:(k + 1) * TN], w, start=True, stop=True)
                    ins.then_inc(s["multiplied"], 1)

                steps(pe, turn)

            @block.scalar
            def _(act):
                def turn(t):
                    act.wait_ge(s["turned"], t + 1)
                    wait(act, s["multiplied"], t)
                    act.activation(xt[0:D, 0:CUT], ps_t[0:D, 0:CUT], ACT.Copy)
                    act.activation(xt[0:D, CUT:SN], ps_t[0:D, 512:512 + TN], ACT.Copy).then_inc(s["turned_copied"], 1)
                    act.wait_ge(s["multiplied"], t + 1)
                    act.wait_ge(s["kv_copied"], t + 1)
                    wait(act, s["stored"], t * 32)
                    act.activation(rows[:, :, 2 * D:], ps_r[0:TN, :, 2 * D:3 * D], ACT.Copy).then_inc(s["q_copied"], 1)

                steps(act, turn)

            @block.vector
            def _(dve):
                dve.memset(xt[D:D + 1, :], 1.0).then_inc(s["ones_made"], 1)
                def turn(t):
                    dve.wait_ge(s["multiplied"], t + 1)
                    wait(dve, s["stored"], t * 32)
                    dve.tensor_copy(rows[:, :, 0:2 * D], ps_r[0:TN, :, 0:2 * D]).then_inc(s["kv_copied"], 1)

                steps(dve, turn)
        clear_semaphores(nc, s)


def edge_keys(nc, c, A):
    with ExitStack() as ctx:
        s = semaphores(nc, ctx, ["loaded", "chain", "made", "stored"], "keys")
        src_i = ctx.enter_context(sbuf(nc, "src_i", [P, NB * COLS], I32))
        src_f = ctx.enter_context(sbuf(nc, "src_f", [P, NB * COLS], F32))
        tile_f = ctx.enter_context(sbuf(nc, "tile_f", [P, NB * COLS], F32))
        tile_i = ctx.enter_context(sbuf(nc, "tile_i", [P, NB * COLS], I32))
        keys = ctx.enter_context(sbuf(nc, "keys", [P, NB * COLS, 2], F32))
        with nc.Block() as block:
            @block.sync
            def _(sp):
                sp.dma_start(src_i[:, :], A["src"].rearrange("b p g -> p b g")).then_inc(s["loaded"], 16)
                sp.wait_ge(s["made"], 1)
                sp.dma_start(c.edge_keys.rearrange("(b p g) a -> p b (g a)", p=P, g=COLS),
                             keys[:, :, :].rearrange("p (b g) a -> p b (g a)", g=COLS)).then_inc(s["stored"], 16)
                sp.wait_ge(s["stored"], 16)

            @block.vector
            def _(dve):
                dve.wait_ge(s["loaded"], 16)
                ch = Chain(dve, s["chain"])
                ch.then(dve.tensor_copy(src_f[:, :], src_i[:, :]))
                ch.then(dve.tensor_scalar(tile_f[:, :], src_f[:, :], -(TN - 1) / 2, 1.0 / TN, ALU.add, ALU.mult))
                ch.then(dve.tensor_copy(tile_i[:, :], tile_f[:, :]))
                ch.then(dve.tensor_copy(tile_f[:, :], tile_i[:, :]))
                dve.scalar_tensor_tensor(out=keys[:, :, 1], in0=tile_f[:, :], scalar=float(-TN), in1=src_f[:, :],
                                         op0=ALU.mult, op1=ALU.add)
                ch.then(dve.scalar_tensor_tensor(out=keys[:, :, 0], in0=c.dst_f[:, :], scalar=float(TILES),
                                                 in1=tile_f[:, :], op0=ALU.mult, op1=ALU.add))
                dve.sem_inc(s["made"], 1)
        clear_semaphores(nc, s)


def group_starts(nc, c):
    with ExitStack() as ctx:
        s = semaphores(nc, ctx, ["moved", "chain"], "starts")
        counts = ctx.enter_context(sbuf(nc, "counts", [1, N], F32))
        ends = ctx.enter_context(sbuf(nc, "ends", [1, N], F32))
        with nc.Block() as block:
            @block.sync
            def _(sp):
                sp.dma_start(counts[:, :], c.sums[MROWS - 1:MROWS, 0:N]).then_inc(s["moved"], 16)

            @block.vector
            def _(dve):
                ch = Chain(dve, s["chain"])
                if GROUPS > N // GROUP:
                    dve.memset(c.starts[:, N // GROUP:], 0)
                ch.then(dve.memset(c.starts[:, 0:1], 0))
                dve.wait_ge(s["moved"], 16)
                ch.then(dve.tensor_tensor_scan(ends[:, :], counts[:, :], counts[:, :], 0.0, ALU.add, ALU.max))
                dve.tensor_copy(c.starts[:, 1:N // GROUP],
                                ends[:, :].rearrange("p (g d) -> p g d", d=GROUP)[:, 0:N // GROUP - 1, GROUP - 1])
        clear_semaphores(nc, s)


def build_adjacency(nc, c):
    names = ["even_loaded", "odd_loaded", "made", "counted"]
    with ExitStack() as ctx:
        s = semaphores(nc, ctx, [f"{n}{i}" for n in names for i in range(SLOTS)] + [f"copied{i}" for i in range(BANKS)]
                       + ["stored0", "stored1", "begun", "begun_act", "begun_sp", "iota_made", "chain", "reduced", "checked",
                          "converted"], "adjacency")
        even_loaded, odd_loaded, made, counted = ([s[f"{n}{i}"] for i in range(SLOTS)] for n in names)
        copied = [s[f"copied{i}"] for i in range(BANKS)]
        stored = [s["stored0"], s["stored1"]]
        loaded = [even_loaded, odd_loaded]

        def sb(name, shape, dt=F32):
            return ctx.enter_context(sbuf(nc, name, shape, dt))

        wide = max(GROUP * TILES, TN)
        strip = sb("strip", [TN, 2, TILES, CHUNK], F8)
        iota = sb("iota_h", [P, wide], F16)
        first_key = c.rel[:, 0:GROUPS]
        keys = c.base_f[:, 0:2 * SLOTS * GCOLS * 2].rearrange("p (e s j a) -> p e s j a", e=2, s=SLOTS, j=GCOLS)
        by_key = sb("by_key", [P, SLOTS, GCOLS, GROUP * TILES], BF16)
        by_row = sb("by_row", [P, SLOTS, GCOLS, TN], BF16)
        integers = by_key[:, :, :, :].rearrange("p s j k -> p (s j k)").bitcast(I32)
        first_i, iota_i = integers[:, 0:GROUPS], integers[:, GROUPS:GROUPS + wide]
        found = c.y_nodes[:, 0:2, 0:CHUNK // PAIR]
        totals = c.y_nodes[:, 2, 0:4]
        ones = c.y_nodes[:, 2, 4:5]
        ps = ctx.enter_context(psum(nc, "ps_pair", [P, BANKS, 512], F32))
        ps_sum = ctx.enter_context(psum(nc, "ps_total", [P, 512], F32))
        PAIRS_IN = CHUNK // PAIR
        TURNS = PAIRS_IN // BANKS

        with nc.Block() as block:
            @block.sync
            def _(sp):
                def strip_turn(k, parity):
                    with sp.Fori(0, TURNS // 2) as i:
                        _, starts = nc.values_load_multi_w_load_instructions(
                            c.starts[0:1, ds((k * TURNS + 2 * i) * SLOTS, 2 * SLOTS)], engines=[mybir.EngineType.SP],
                            min_val=0, max_val=E)
                        for odd in range(2):
                            turn = k * TURNS + 2 * i + odd
                            for slot, start in enumerate(starts[odd * SLOTS:(odd + 1) * SLOTS]):
                                sp.wait_ge(made[slot], 2 * turn + 2)
                                sp.dma_start(keys[:, odd, slot, :, :].rearrange("p j a -> p (j a)"),
                                             c.edge_keys[ds(start, GCAP), :].rearrange("(p j) a -> p (j a)", j=GCOLS))\
                                    .then_inc(loaded[odd][slot], 16)
                    sp.wait_ge(copied[BANKS - 1], (k + 1) * TURNS + 1)
                    sp.sem_inc(s["begun_sp"], 1)
                    sp.dma_start(c.adjacency[ds(k, 1)].rearrange("a h p f -> p (a h) f"),
                                 strip[:, parity, :, :].rearrange("p (h t) d -> p h (t d)", h=2).bitcast(U8))\
                        .then_inc(stored[parity], 16)

                strip_turn(0, 0)
                with sp.Fori(0, (CHUNKS - 1) // 2) as i:
                    strip_turn(2 * i + 1, 1)
                    strip_turn(2 * i + 2, 0)
                sp.wait_ge(stored[0], 16 * ((CHUNKS + 1) // 2))
                sp.wait_ge(stored[1], 16 * (CHUNKS // 2))

            @block.gpsimd
            def _(pool):
                pool.iota(iota_i, pattern=[[1, wide]], base=0, channel_multiplier=0)\
                    .then_inc(s["iota_made"], 1)
                pool.iota(first_i[:, :], pattern=[[-GROUP * TILES // 2, GROUPS]], base=0, channel_multiplier=0)\
                    .then_inc(s["iota_made"], 1)
                pool.wait_ge(s["converted"], 1)
                with pool.Fori(0, GROUPS // SLOTS // 2) as u:
                    for odd in range(2):
                        for slot in range(SLOTS):
                            pool.wait_ge(loaded[odd][slot], u * 16 + 16)
                            pool.wait_ge(counted[slot], 2 * u + odd + 1)
                            pool.sem_inc(s["begun"], 1)
                            pool.tensor_scalar(by_row[:, slot, 1, :], iota[:, 0:TN], keys[:, odd, slot, 1, 1:2], None,
                                               ALU.is_equal).then_inc(made[slot], 1)

            @block.vector
            def _(dve):
                ch = Chain(dve, s["chain"])
                dve.memset(ones[:, :], 1.0)
                dve.memset(totals[:, :], 0.0)
                dve.wait_ge(s["iota_made"], 2)
                dve.tensor_copy(iota[:, :], iota_i[:, :])
                ch.then(dve.tensor_scalar(first_key[:, :], first_i[:, :], -2.0, None, ALU.mult))
                dve.sem_inc(s["converted"], 1)
                for slot in range(SLOTS):
                    dve.sem_inc(made[slot], 4)

                def strip_turn(k, parity):
                    with dve.Fori(0, TURNS // 2) as i:
                        for odd in range(2):
                            turn = k * TURNS + 2 * i + odd
                            for slot in range(SLOTS):
                                g = turn * SLOTS + slot
                                dve.wait_ge(loaded[odd][slot], (k * (TURNS // 2) + i) * 16 + 16)
                                dve.wait_ge(counted[slot], turn + 1)
                                for j in range(GCOLS):
                                    dve.tensor_scalar(by_key[:, slot, j, :], iota[:, 0:GROUP * TILES],
                                                      first_key[:, ds(g, 1)], keys[:, odd, slot, j, 0:1],
                                                      ALU.add, ALU.is_equal)
                                dve.tensor_scalar(by_row[:, slot, 0, :], iota[:, 0:TN], keys[:, odd, slot, 0, 1:2], None,
                                                  ALU.is_equal).then_inc(made[slot], 1)
                    dve.wait_ge(copied[BANKS - 1], (k + 1) * TURNS + 1)
                    for n, op in ((2, ALU.max), (3, ALU.add)):
                        dve.tensor_reduce(totals[:, n:n + 1], found[:, parity, :], AX_X, op)
                    dve.drain().then_inc(s["reduced"], 1)
                    dve.tensor_tensor(totals[:, 0:1], totals[:, 0:1], totals[:, 2:3], ALU.max)
                    dve.tensor_tensor(totals[:, 1:2], totals[:, 1:2], totals[:, 3:4], ALU.add)
                    dve.drain()

                strip_turn(0, 0)
                with dve.Fori(0, (CHUNKS - 1) // 2) as i:
                    strip_turn(2 * i + 1, 1)
                    strip_turn(2 * i + 2, 0)
                dve.tensor_scalar(totals[:, 0:1], totals[:, 0:1], float(EXACT), None, ALU.is_le)
                dve.drain().then_inc(s["checked"], 1)
                dve.wait_ge(s["checked"], 2)
                dve.tensor_scalar(c.dense_f[:, 0:1], ps_sum[0:1, 0:1], float(TN), None, ALU.is_equal)
                dve.tensor_scalar(c.dense_f[:, 1:2], ps_sum[0:1, 1:2], float(E), None, ALU.is_equal)
                dve.drain()
                dve.tensor_tensor(c.dense_f[:, 2:3], c.dense_f[:, 0:1], c.dense_f[:, 1:2], ALU.mult)
                dve.drain()
                dve.tensor_copy(c.dense[:, :], c.dense_f[:, 2:3])

            @block.tensor
            def _(pe):
                for slot in range(SLOTS):
                    pe.sem_inc(counted[slot], 1)
                with pe.Fori(0, GROUPS // SLOTS) as u:
                    for slot in range(SLOTS):
                        pe.wait_ge(made[slot], 2 * u + 6)
                        if slot % 2 == 0:
                            pe.wait_ge(copied[slot // 2], u + 1)
                        at = (slot % 2) * GROUP * TILES
                        for j in range(GCOLS):
                            ins = pe.matmul(ps[0:TN, slot // 2, at:at + GROUP * TILES], by_row[:, slot, j, :],
                                            by_key[:, slot, j, :], start=(j == 0), stop=(j == GCOLS - 1))
                        ins.then_inc(counted[slot], 1)
                pe.wait_ge(s["checked"], 1)
                pe.matmul(ps_sum[0:1, 0:2], ones[:, :], totals[:, 0:2], start=True, stop=True).then_inc(s["checked"], 1)

            @block.scalar
            def _(act):
                for h in range(BANKS):
                    act.sem_inc(copied[h], 1)

                def strip_turn(k, parity, before):
                    wait(act, stored[parity], before * 16)
                    if not isinstance(k, int) or k > 1:
                        act.wait_ge(s["reduced"], k - 1)
                    for q in range(PAIRS_IN):
                        h = q % BANKS
                        act.wait_ge(counted[2 * h + 1], k * TURNS + q // BANKS + 2)
                        act.sem_inc(s["begun_act"], 1)
                        act.activation(strip[:, parity, :, q * PAIR:(q + 1) * PAIR],
                                       ps[0:TN, h, 0:PAIR * TILES].rearrange("p (d t) -> p t d", t=TILES), ACT.Copy,
                                       saturate=False, accum_out=found[:, parity, q:q + 1]).then_inc(copied[h], 1)

                strip_turn(0, 0, 0)
                strip_turn(1, 1, 0)
                strip_turn(2, 0, 1)
                with act.Fori(1, (CHUNKS - 1) // 2) as i:
                    strip_turn(2 * i + 1, 1, i)
                    strip_turn(2 * i + 2, 0, i + 1)
        clear_semaphores(nc, s)


def split_rows(nc, c, rows, parts):
    with ExitStack() as ctx:
        s = semaphores(nc, ctx, ["high", "left1", "middle", "left2"], "split")
        left = ctx.enter_context(sbuf(nc, "left", [TN, TILES, D], F32))
        cuts = [slice(k, k + TILES // 5) for k in range(0, TILES, TILES // 5)]
        with nc.Block() as block:
            @block.scalar
            def _(act):
                for at in cuts:
                    act.activation(parts[:, at, 0, :], rows[:, at, :], ACT.Copy).then_inc(s["high"], 1)
                for n, at in enumerate(cuts):
                    act.wait_ge(s["left1"], n + 1)
                    act.activation(parts[:, at, 1, :], left[:, at, :], ACT.Copy).then_inc(s["middle"], 1)
                for n, at in enumerate(cuts):
                    act.wait_ge(s["left2"], n + 1)
                    act.activation(parts[:, at, 2, :], left[:, at, :], ACT.Copy)

            @block.vector
            def _(dve):
                for n, at in enumerate(cuts):
                    dve.wait_ge(s["high"], n + 1)
                    dve.tensor_tensor(left[:, at, :], rows[:, at, :], parts[:, at, 0, :], ALU.subtract)\
                        .then_inc(s["left1"], 1)
                for n, at in enumerate(cuts):
                    dve.wait_ge(s["middle"], n + 1)
                    dve.tensor_tensor(left[:, at, :], left[:, at, :], parts[:, at, 1, :], ALU.subtract)\
                        .then_inc(s["left2"], 1)
        clear_semaphores(nc, s)


def dense_pass(nc, c, rows):
    with ExitStack() as ctx:
        parts = ctx.enter_context(sbuf(nc, "parts", [TN, TILES, 3, D], BF16))
        split_rows(nc, c, rows, parts)
        s = semaphores(nc, ctx, ["loaded0", "loaded1", "used0", "used1", "begun_sp", "begun_pe"]
                       + [f"{n}{q}" for n in ("multiplied", "added", "turned", "kept") for q in range(DTILES)], "dense")
        loaded, used = ([s[n + "0"], s[n + "1"]] for n in ("loaded", "used"))
        multiplied, added, turned, kept = ([s[f"{n}{q}"] for q in range(DTILES)]
                                           for n in ("multiplied", "added", "turned", "kept"))
        strip = ctx.enter_context(sbuf(nc, "half_strips", [TN, 2, HALF, CHUNK], F8))
        whole = ctx.enter_context(sbuf(nc, "whole", [TN, DTILES, D], F32))
        ps = ctx.enter_context(psum(nc, "ps_parts", [P, DTILES, 512], F32))
        ps_t = ctx.enter_context(psum(nc, "ps_turned", [P, 2, 512], F32))

        def strips(eng, body):
            body(0)
            with eng.Fori(1, CHUNKS) as k:
                body(k)

        with nc.Block() as block:
            @block.sync
            def _(sp):
                def turn(k):
                    for h in range(2):
                        wait(sp, used[h], k)
                        sp.sem_inc(s["begun_sp"], 1)
                        sp.dma_start(strip[:, h, :, :].rearrange("p t d -> p (t d)").bitcast(U8),
                                     c.adjacency[ds(k, 1), h].rearrange("a p f -> (a p) f")).then_inc(loaded[h], 16)

                strips(sp, turn)

            @block.tensor
            def _(pe):
                def turn(k):
                    def turn_tile(q):
                        pe.wait_ge(added[q], k + 1)
                        if q < 2:
                            wait(pe, kept[q + 2], k)
                        else:
                            pe.wait_ge(kept[q - 2], k + 1)
                        pe.transpose(ps_t[0:D, q % 2, 0:TN], whole[:, q, :], c.ident[0:TN, 0:TN]).then_inc(turned[q], 1)

                    for h in range(2):
                        pe.wait_ge(loaded[h], k * 16 + 16)
                        pe.sem_inc(s["begun_pe"], 1)
                        for q in range(DTILES):
                            if h == 0:
                                wait(pe, added[q], k)
                                pe.sem_inc(s["begun_pe"], 1)
                            for t in range(HALF):
                                ins = pe.matmul(ps[0:TN, q, 0:3 * D], strip[:, h, t, q * TN:(q + 1) * TN],
                                                parts[:, h * HALF + t, :, :].rearrange("p a f -> p (a f)"),
                                                start=(h == 0 and t == 0), stop=(h == 1 and t == HALF - 1))
                            if h == 1:
                                ins.then_inc(multiplied[q], 1)
                                if q > 0:
                                    turn_tile(q - 1)
                            elif q == DTILES - 1:
                                ins.then_inc(used[h], 1)
                    turn_tile(DTILES - 1)
                    pe.sem_inc(used[1], 1)

                strips(pe, turn)

            @block.vector
            def _(dve):
                def turn(k):
                    for q in range(DTILES):
                        dve.wait_ge(multiplied[q], k + 1)
                        wait(dve, turned[q], k)
                        dve.tensor_reduce(whole[:, q, :], ps[0:TN, q, 0:3 * D].rearrange("p (a f) -> p f a", a=3),
                                          AX_X, ALU.add).then_inc(added[q], 1)

                strips(dve, turn)

            @block.scalar
            def _(act):
                def turn(k):
                    for q in range(DTILES):
                        act.wait_ge(turned[q], k + 1)
                        act.activation(c.sums[0:D, ds(k * CHUNK + q * TN, TN)], ps_t[0:D, q % 2, 0:TN], ACT.Copy)\
                            .then_inc(kept[q], 1)

                strips(act, turn)
        clear_semaphores(nc, s)


def place_windows(nc, c):
    with ExitStack() as ctx:
        s = semaphores(nc, ctx, ["chain"], "windows")
        with nc.Block() as block:
            @block.vector
            def _(dve):
                ch = Chain(dve, s["chain"])
                ch.then(dve.tensor_scalar(c.base_f[:, :], c.first_dst[:, :], c.sorted_[:, 0:1], c.round_base[:, 0:1],
                                          ALU.mult, ALU.add))
                dve.tensor_copy(c.base_i[:, :], c.base_f[:, :])
                dve.tensor_tensor(c.rel[:, 0:NB * COLS].rearrange("p (b g) -> p b g", g=COLS),
                                  c.dst_f[:, :].rearrange("p (b g) -> p b g", g=COLS),
                                  c.base_f[:, :].unsqueeze(2).to_broadcast([P, NB, COLS]), ALU.subtract)
                ch.then(dve.tensor_scalar(c.round_base[:, :], c.round_base[:, :], float(WIN), None, ALU.add))
        clear_semaphores(nc, s)


def edge_pass(nc, c, A, kind, table):
    attend, relu = kind == "attend", kind == "relu"
    rows = MROWS if attend else D
    wide = 2 * D if attend else D
    names = ["idx_loaded0", "idx_loaded1", "attr_loaded0", "attr_loaded1", "q_loaded0", "q_loaded1", "onehot_made0",
             "onehot_made1", "attr_turned", "attr_copied", "onehot_turned", "onehot_copied", "turned0", "turned1",
             "eq_ready", "eq_used", "score_ready", "exp_done", "msg_made0", "msg_made1", "sum_made0", "sum_made1",
             "seg_done0", "seg_done1", "added0", "added1", "gathered0", "gathered1", "begun", "chain", "set_up"]
    with ExitStack() as outer, ExitStack() as ctx:
        s = semaphores(nc, outer, names, kind)
        outer.callback(clear_gather_semaphores, nc, s)

        def two(name):
            return [s[name + "0"], s[name + "1"]]

        idx_loaded, attr_loaded, q_loaded, onehot_made = map(two, ("idx_loaded", "attr_loaded", "q_loaded", "onehot_made"))
        turned, msg_made, sum_made, seg_done, added = map(two, ("turned", "msg_made", "sum_made", "seg_done", "added"))
        gathered = two("gathered")

        def sb(name, shape):
            return ctx.enter_context(sbuf(nc, name, shape, F32))

        idx = ctx.enter_context(sbuf(nc, "idx", [P, 2, COLS], I32))
        got = sb("got", [P, 2, COLS, wide])
        onehot = sb("onehot", [P, 2, COLS, WIN])
        ps_seg = ctx.enter_context(psum(nc, "ps_seg", [P, 2, 512], F32))
        if kind != "plain":
            attr = sb("attr", [P, 2, COLS, D])
            msg = sb("msg", [P, 2, COLS, rows])
        if relu:
            total = sb("total", [P, 2, COLS, D])
        if attend:
            q_win = sb("q_win", [WIN, 2, D])
            attr_t = sb("attr_t", [D + 1, 2, SUB * P])
            onehot_t = sb("onehot_t", [WIN, 2, SUB * P])
            key_edge = sb("key_edge", [P, COLS, D])
            prod = sb("prod", [P, COLS, D])
            score = sb("score", [P, COLS, H])
            clipped = sb("clipped", [P, COLS, H])
            ps_at = ctx.enter_context(psum(nc, "ps_at", [P, 512], F32))
            ps_oh = ctx.enter_context(psum(nc, "ps_oh", [P, 512], F32))
            ps_e = ctx.enter_context(psum(nc, "ps_e", [P, 2, 512], F32))
            ps_q = ctx.enter_context(psum(nc, "ps_q", [P, 2, 512], F32))
        block = ctx.enter_context(nc.Block())
        src_d, attr_d = A["src"], A["edge_attr_96"]
        attr_full = attr_d[0:FULL * EPB, :].rearrange("(b p g) f -> b p (g f)", p=P, g=COLS)

        def before(i, slot):
            return 1 - slot, (i + 1 if slot else i)

        def pairs(eng, turn):
            for i in range(2):
                for slot in range(2):
                    turn(i, slot, i == 0 and slot == 0, False)
            with eng.Fori(2, PAIRS - 1) as i:
                for slot in range(2):
                    turn(i, slot, False, False)
            for slot in range(2):
                turn(PAIRS - 1, slot, False, slot == 1)

        @block.sync
        def _(sp):
            def loads(i, slot, is_first, is_last):
                b = 2 * i + slot
                wait(sp, gathered[slot], i * GATHERED)
                sp.dma_start(idx[:, slot, :], src_d[ds(b, 1)].rearrange("a p g -> (a p) g")).then_inc(idx_loaded[slot], 16)
                if kind != "plain":
                    if attend:
                        wait(sp, turned[slot], i)
                    else:
                        wait(sp, sum_made[slot], i)
                    if not is_last:
                        sp.dma_start(attr[:, slot, :, :].rearrange("p g f -> p (g f)"),
                                     attr_full[ds(b, 1)].rearrange("a p f -> (a p) f")).then_inc(attr_loaded[slot], 16)
                    else:
                        rest = attr_d[FULL * EPB:E, :]
                        whole, part = REST // COLS, REST % COLS
                        sp.dma_start(attr[0:whole, slot, :, :].rearrange("p g f -> p (g f)"),
                                     rest[0:whole * COLS, :].rearrange("(p g) f -> p (g f)", g=COLS))\
                            .then_inc(attr_loaded[slot], 16)
                        if part:
                            sp.dma_start(attr[whole:whole + 1, slot, 0:part, :].rearrange("p g f -> p (g f)"),
                                         rest[whole * COLS:REST, :].rearrange("(p g) f -> p (g f)", g=part))\
                                .then_inc(attr_loaded[slot], 16)
                if attend:
                    base = sp.value_load(c.base_i[0:1, ds(b, 1)], min_val=0, max_val=N - 1)
                    wait(sp, msg_made[slot], i)
                    sp.dma_start(q_win[:, slot, :], c.q_table[ds(base, WIN), :]).then_inc(q_loaded[slot], 16)

            pairs(sp, loads)

        @block.gpsimd
        def _(pool):
            free = msg_made if attend else sum_made if relu else seg_done

            def gathers(i, slot, is_first, is_last):
                pool.wait_ge(idx_loaded[slot], i * 16 + 16)
                wait(pool, free[slot], i)
                pool.sem_inc(s["begun"], 1)
                for g in range(COLS):
                    pool.indirect_dma_start(got[:, slot, g, :], None, table[:, :],
                                            bass.IndirectOffsetOnAxis(ap=idx[:, slot, g:g + 1], axis=0))\
                        .then_inc(gathered[slot], 16)

            pairs(pool, gathers)

        @block.tensor
        def _(pe):
            def sum_messages(slot, n):
                wait(pe, added[slot], n - 1)
                pe.wait_ge(onehot_made[slot], n)
                if kind == "plain":
                    pe.wait_ge(gathered[slot], n * GATHERED)
                else:
                    pe.wait_ge(msg_made[slot], n)
                of = got if kind == "plain" else msg
                for g in range(COLS):
                    ins = pe.matmul(ps_seg[0:rows, slot, 0:WIN], of[:, slot, g, :], onehot[:, slot, g, :],
                                    start=(g == 0), stop=(g == COLS - 1))
                ins.then_inc(seg_done[slot], 1)

            def products(i, slot, is_first, is_last):
                b = 2 * i + slot
                more = 16 if is_last and REST % COLS else 0
                pe.wait_ge(attr_loaded[slot], i * 16 + 16 + more)
                pe.wait_ge(onehot_made[slot], i + 1)
                for j in range(2):
                    wait(pe, s["attr_copied"], b * 2 + j)
                    for k in range(SUB):
                        ins = pe.transpose(ps_at[0:D, k * P:(k + 1) * P], attr[:, slot, j * SUB + k, :], c.ident[:, :])
                    ins.then_inc(s["attr_turned"], 1)
                    wait(pe, s["onehot_copied"], b * 2 + j)
                    pe.sem_inc(s["begun"], 1)
                    for k in range(SUB):
                        ins = pe.transpose(ps_oh[0:WIN, k * P:(k + 1) * P], onehot[:, slot, j * SUB + k, :], c.ident[:, :])
                    ins.then_inc(s["onehot_turned"], 1)
                pe.wait_ge(q_loaded[slot], i * 16 + 16)
                wait(pe, s["eq_used"], b * 2)
                for j in range(2):
                    pe.wait_ge(s["attr_copied"], b * 2 + 1 + j)
                    pe.wait_ge(s["onehot_copied"], b * 2 + 1 + j)
                    for k in range(SUB):
                        pe.matmul(ps_e[:, j, k * D:(k + 1) * D], attr_t[:, j, k * P:(k + 1) * P], c.w_e[:, :],
                                  start=True, stop=True)
                        ins = pe.matmul(ps_q[:, j, k * D:(k + 1) * D], onehot_t[:, j, k * P:(k + 1) * P], q_win[:, slot, :],
                                        start=True, stop=True)
                    ins.then_inc(s["eq_ready"], 1)
                if not is_first:
                    sum_messages(*before(i, slot))

            if attend:
                pe.wait_ge(s["set_up"], 1)
                pairs(pe, products)
                sum_messages(1, PAIRS)
            else:
                pairs(pe, lambda i, slot, is_first, is_last: sum_messages(slot, i + 1))

        @block.scalar
        def _(act):
            def weights(slot, n, b):
                act.wait_ge(s["score_ready"], b)
                wait(act, seg_done[slot], n - 1)
                act.activation(msg[:, slot, :, D:D + H], clipped[:, :, :], ACT.Exp, scale=HD ** -0.5)\
                    .then_inc(s["exp_done"], 1)

            def copies(i, slot, is_first, is_last):
                b = 2 * i + slot
                wait(act, s["eq_ready"], b * 2)
                for j in range(2):
                    act.wait_ge(s["attr_turned"], b * 2 + 1 + j)
                    ins = act.activation(attr_t[0:D, j, :], ps_at[0:D, :], ACT.Copy).then_inc(s["attr_copied"], 1)
                    if j == 1:
                        act.sem_inc(turned[slot], 1)
                    act.wait_ge(s["onehot_turned"], b * 2 + 1 + j)
                    act.activation(onehot_t[:, j, :], ps_oh[0:WIN, :], ACT.Copy).then_inc(s["onehot_copied"], 1)
                if not is_first:
                    weights(*before(i, slot), b)

            def rectify(i, slot, is_first, is_last):
                act.wait_ge(sum_made[slot], i + 1)
                wait(act, seg_done[slot], i)
                act.activation(msg[:, slot, :, :], total[:, slot, :, :], ACT.Relu).then_inc(msg_made[slot], 1)

            if attend:
                pairs(act, copies)
                weights(1, PAIRS, NB)
            if relu:
                pairs(act, rectify)

        @block.vector
        def _(dve):
            def make_onehot(b, slot):
                rel = c.rel[:, ds(b * COLS, COLS)].unsqueeze(2).to_broadcast([P, COLS, WIN])
                dve.tensor_tensor(onehot[:, slot, :, :], c.iota[:, :].unsqueeze(1).to_broadcast([P, COLS, WIN]),
                                  rel, ALU.is_equal).then_inc(onehot_made[slot], 1)

            def add_sums(b, slot, n):
                base = dve.value_load(c.base_i[0:1, ds(b, 1)], min_val=0, max_val=N - 1)
                wait(dve, added[1 - slot], n if slot else n - 1)
                dve.wait_ge(seg_done[slot], n)
                at = c.sums[0:rows, ds(base, WIN)]
                dve.tensor_tensor(at, at, ps_seg[0:rows, slot, 0:WIN], ALU.add).then_inc(added[slot], 1)

            def turn(i, slot, is_first, is_last):
                b = 2 * i + slot
                if attend:
                    ch = Chain(dve, s["chain"], b, 5)
                    dve.wait_ge(gathered[slot], i * GATHERED + GATHERED)
                    for j in range(2):
                        of = slice(j * SUB, (j + 1) * SUB)
                        dve.wait_ge(s["eq_ready"], b * 2 + 1 + j)
                        ch.then(dve.tensor_tensor(key_edge[:, of, :], got[:, slot, of, 0:D],
                                                  ps_e[:, j, 0:SUB * D].rearrange("p (k f) -> p k f", f=D), ALU.mult))
                        ch.then(dve.tensor_tensor(prod[:, of, :], key_edge[:, of, :],
                                                  ps_q[:, j, 0:SUB * D].rearrange("p (k f) -> p k f", f=D), ALU.mult))
                        dve.sem_inc(s["eq_used"], 1)
                    ch.then(dve.tensor_reduce(score[:, :, :], prod[:, :, :].rearrange("p g (h d) -> p g h d", d=HD),
                                              AX_X, ALU.add))
                    dve.tensor_scalar(clipped[:, :, :], score[:, :, :], CLIP, -CLIP, ALU.min, ALU.max)\
                        .then_inc(s["score_ready"], 1)
                if relu:
                    more = 16 if is_last and REST % COLS else 0
                    dve.wait_ge(gathered[slot], i * GATHERED + GATHERED)
                    dve.wait_ge(attr_loaded[slot], i * 16 + 16 + more)
                    wait(dve, msg_made[slot], i)
                    dve.tensor_tensor(total[:, slot, :, :], got[:, slot, :, :], attr[:, slot, :, :], ALU.add)\
                        .then_inc(sum_made[slot], 1)
                old, n = before(i, slot)
                if not is_first:
                    add_sums(b - 1, old, n)
                if not is_last:
                    make_onehot(b + 1, old)
                if attend:
                    dve.wait_ge(s["exp_done"], b + 1)
                    dve.tensor_tensor(msg[:, slot, :, 0:D].rearrange("p g (h d) -> p g h d", d=HD),
                                      got[:, slot, :, D:2 * D].rearrange("p g (h d) -> p g h d", d=HD),
                                      msg[:, slot, :, D:D + H].unsqueeze(3).to_broadcast([P, COLS, H, HD]),
                                      ALU.mult).then_inc(msg_made[slot], 1)

            if attend:
                ch = Chain(dve, s["set_up"])
                dve.memset(attr_t[D:D + 1, :, :], 1.0)
                dve.memset(msg[:, :, :, MROWS - 1:MROWS], 1.0)
                dve.drain().then_inc(s["set_up"], 1)
            make_onehot(0, 0)
            pairs(dve, turn)
            add_sums(NB - 1, 1, PAIRS)



def layer_norm(dve, ch, c, s, t, n, h, out):
    for k in range(ST):
        ins = dve.bn_stats(n.stats[:, k, :], h[:, k, :])
    ch.then(ins)
    dve.sem_inc(s["taken"], 1)
    for k in range(ST):
        ins = dve.bn_aggr(n.moments[:, k, :], n.stats[:, k, :])
    ins.then_inc(s["var_ready"], 1)
    dve.wait_ge(s["root_ready"], t + 1)
    ch.then(dve.reciprocal(n.rstd[:, :], n.root[:, :]))
    for k in range(ST):
        ins = dve.tensor_scalar(out[:, k, :], h[:, k, :], n.moments[:, k, 0:1], n.rstd[:, k:k + 1],
                                ALU.subtract, ALU.mult)
    return ins


def root_of_var(act, c, s, t, n):
    act.wait_ge(s["var_ready"], t + 1)
    act.activation(n.root[:, :], n.moments[:, :, 1], ACT.Sqrt, bias=c.eps[0:TN, 0:1]).then_inc(s["root_ready"], 1)


class Norm:
    def __init__(self, nc, ctx):
        def sb(name, shape):
            return ctx.enter_context(sbuf(nc, name, shape, F32))

        self.stats = sb("ln_stats", [TN, ST, 6])
        self.moments = sb("ln_moments", [TN, ST, 2])
        self.root = sb("ln_root", [TN, ST])
        self.rstd = sb("ln_rstd", [TN, ST])


def step_rows(table, t):
    return table.rearrange("(t k p) f -> t p k f", k=ST, p=TN)[ds(t, 1)].rearrange("a p k f -> (a p) k f")


def store_steps(sp, s, table, rows):
    def turn(t):
        sp.wait_ge(s["rows_ready"], t + 1)
        sp.dma_start(step_rows(table, t), rows).then_inc(s["stored"], 16)

    steps(sp, turn)
    sp.wait_ge(s["stored"], 16 * STEPS)


def span(t):
    return ds(t * SN, SN)


def psum_tile_at(k):
    return k * TN if k < 4 else 512


def after_attention(nc, c, table):
    with ExitStack() as ctx:
        s = semaphores(nc, ctx, ["sums_copied", "turned", "var_ready", "taken", "root_ready", "rows_ready", "stored", "chain",
                           "kept"], "attention")
        sums_step = ctx.enter_context(sbuf(nc, "sums_step", [MROWS, SN], F32))
        h = ctx.enter_context(sbuf(nc, "h", [TN, ST, D], F32))
        rows = ctx.enter_context(sbuf(nc, "rows", [TN, ST, D], F32))
        z = ctx.enter_context(sbuf(nc, "z", [TN, ST, H], F32))
        zr = ctx.enter_context(sbuf(nc, "zr", [TN, ST, H], F32))
        ps = ctx.enter_context(psum(nc, "ps", [P, 2 * 512], F32))
        psk = ps[0:TN, 0:ST * P].rearrange("p (k f) -> p k f", f=P)
        n = Norm(nc, ctx)
        with nc.Block() as block:
            @block.sync
            def _(sp):
                store_steps(sp, s, table, rows[:, :, :])

            @block.scalar
            def _(act):
                def turn(t):
                    wait(act, s["turned"], t)
                    act.activation(sums_step[:, :], c.sums[0:MROWS, span(t)], ACT.Copy).then_inc(s["sums_copied"], 1)
                    root_of_var(act, c, s, t, n)
                    act.wait_ge(s["rows_ready"], t + 1)
                    act.activation(c.x_nodes[:, ds(t * ST, ST), :], rows[:, :, :], ACT.Copy).then_inc(s["kept"], 1)

                steps(act, turn)

            @block.tensor
            def _(pe):
                def turn(t):
                    pe.wait_ge(s["sums_copied"], t + 1)
                    wait(pe, s["rows_ready"], t)
                    for k in range(ST):
                        ins = pe.transpose(ps[0:TN, k * P:k * P + MROWS], sums_step[:, k * TN:(k + 1) * TN],
                                           c.ident[0:MROWS, 0:MROWS])
                    ins.then_inc(s["turned"], 1)

                steps(pe, turn)

            @block.vector
            def _(dve):
                def turn(t):
                    ch = Chain(dve, s["chain"], t, 7)
                    dve.wait_ge(s["turned"], t + 1)
                    dve.tensor_copy(c.deg[:, ds(t * ST, ST)], psk[:, :, MROWS - 1])
                    ch.then(dve.tensor_scalar(z[:, :, :], psk[:, :, D:D + H], 1e-6, None, ALU.add))
                    ch.then(dve.reciprocal(zr[:, :, :], z[:, :, :]))
                    ch.then(dve.tensor_tensor(h[:, :, :].rearrange("p k (h d) -> p k h d", d=HD),
                                              psk[:, :, 0:D].rearrange("p k (h d) -> p k h d", d=HD),
                                              zr[:, :, :].unsqueeze(3).to_broadcast([TN, ST, H, HD]), ALU.mult))
                    ch.then(dve.tensor_tensor(h[:, :, :], h[:, :, :], c.x_nodes[:, ds(t * ST, ST), :], ALU.add))
                    wait(dve, s["stored"], t * 16)
                    wait(dve, s["kept"], t)
                    ins = layer_norm(dve, ch, c, s, t, n, h, rows)
                    ins.then_inc(s["rows_ready"], 1)
                    ch.then(dve.memset(z[:, :, :], 0.0))

                steps(dve, turn)
        clear_semaphores(nc, s)
        s2 = semaphores(nc, ctx, ["chain", "plus_one", "rooted"], "degree")
        d1 = ctx.enter_context(sbuf(nc, "d1", [TN, TILES], F32))
        d2 = ctx.enter_context(sbuf(nc, "d2", [TN, TILES], F32))
        with nc.Block() as block:
            @block.vector
            def _(dve):
                dve.tensor_scalar(d1[:, :], c.deg[:, :], 1.0, 1.0, ALU.add, ALU.max).then_inc(s2["plus_one"], 1)
                dve.wait_ge(s2["rooted"], 1)
                dve.reciprocal(c.dis[:, :], d2[:, :])

            @block.scalar
            def _(act):
                act.wait_ge(s2["plus_one"], 1)
                act.activation(d2[:, :], d1[:, :], ACT.Sqrt).then_inc(s2["rooted"], 1)
        clear_semaphores(nc, s2)


def clear_sums(nc, c):
    with ExitStack() as ctx:
        s = semaphores(nc, ctx, ["chain"], "clear")
        with nc.Block() as block:
            @block.vector
            def _(dve):
                ch = Chain(dve, s["chain"])
                dve.memset(c.sums[0:D, :], 0.0)
                ch.then(dve.memset(c.round_base[:, :], 0.0))
        clear_semaphores(nc, s)


def after_mean(nc, c, table):
    with ExitStack() as outer:
        ht = outer.enter_context(sbuf(nc, "ht", [D, N], F32))
        stats = outer.enter_context(sbuf(nc, "bn_stats", [D, STEPS * 2, 6], F32))
        with ExitStack() as ctx:
            s = semaphores(nc, ctx, ["x_copied", "counts", "turned", "turned_copied", "mean_ready", "multiplied", "h_ready",
                               "stats_done", "chain"], "mean")
            xs = ctx.enter_context(sbuf(nc, "xs", [TN, ST, D], F32))
            xt = ctx.enter_context(sbuf(nc, "xt", [D, SN], F32))
            inv = ctx.enter_context(sbuf(nc, "inv", [D, SN], F32))
            deg = ctx.enter_context(sbuf(nc, "deg_step", [D, SN], F32))
            mean = ctx.enter_context(sbuf(nc, "mean_step", [D, SN], F32))
            ps_t = ctx.enter_context(psum(nc, "ps_t", [P, 1024], F32))
            ps_d = ctx.enter_context(psum(nc, "ps_d", [P, 1024], F32))
            ps_h = ctx.enter_context(psum(nc, "ps_h", [P, 1024], F32))
            with nc.Block() as block:
                @block.scalar
                def _(act):
                    def turn(t):
                        wait(act, s["turned"], t)
                        act.activation(xs[:, :, :], c.x_nodes[:, ds(t * ST, ST), :], ACT.Copy).then_inc(s["x_copied"], 1)
                        act.wait_ge(s["turned"], t + 1)
                        wait(act, s["multiplied"], t)
                        for i, (a, q, w) in enumerate(PIECES):
                            ins = act.activation(xt[:, a:a + w], ps_t[0:D, q:q + w], ACT.Copy)
                        ins.then_inc(s["turned_copied"], 1)
                        act.wait_ge(s["multiplied"], t + 1)
                        for a, q, w in PIECES:
                            ins = act.activation(ht[:, ds(t * SN + a, w)], ps_h[0:D, q:q + w], ACT.Identity,
                                                 bias=c.b_l[:, 0:1])
                        ins.then_inc(s["h_ready"], 1)

                    steps(act, turn)

                @block.tensor
                def _(pe):
                    def turn(t):
                        wait(pe, s["mean_ready"], t)
                        for a, q, w in PIECES:
                            ins = pe.matmul(ps_d[0:D, q:q + w], c.count_row[0:MROWS, :], c.sums[0:MROWS, ds(t * SN + a, w)],
                                            start=True, stop=True)
                        ins.then_inc(s["counts"], 1)
                        pe.wait_ge(s["x_copied"], t + 1)
                        wait(pe, s["turned_copied"], t)
                        for k in range(ST):
                            q = psum_tile_at(k)
                            ins = pe.transpose(ps_t[0:D, q:q + TN], xs[:, k, :], c.ident[0:TN, 0:TN])
                        ins.then_inc(s["turned"], 1)
                        pe.wait_ge(s["turned_copied"], t + 1)
                        pe.wait_ge(s["mean_ready"], t + 1)
                        wait(pe, s["h_ready"], t)
                        for a, q, w in PIECES:
                            pe.matmul(ps_h[0:D, q:q + w], c.w_l[:, :], mean[:, a:a + w], start=True, stop=False)
                            ins = pe.matmul(ps_h[0:D, q:q + w], c.w_r[:, :], xt[:, a:a + w], start=False, stop=True)
                        ins.then_inc(s["multiplied"], 1)

                    steps(pe, turn)

                @block.vector
                def _(dve):
                    def turn(t):
                        ch = Chain(dve, s["chain"], t, 2)
                        dve.wait_ge(s["counts"], t + 1)
                        for a, q, w in PIECES:
                            ins = dve.tensor_scalar(deg[:, a:a + w], ps_d[0:D, q:q + w], 1.0, None, ALU.max)
                        ch.then(ins)
                        ch.then(dve.reciprocal(inv[:, :], deg[:, :]))
                        wait(dve, s["multiplied"], t)
                        dve.tensor_tensor(mean[:, :], c.sums[0:D, span(t)], inv[:, :], ALU.mult).then_inc(s["mean_ready"], 1)
                        dve.wait_ge(s["h_ready"], t + 1)
                        for i, (a, q, w) in enumerate(PIECES):
                            dve.bn_stats(stats[:, ds(t * 2 + i, 1), :].rearrange("p a b -> p (a b)"),
                                         ht[:, ds(t * SN + a, w)])

                    steps(dve, turn)
            clear_semaphores(nc, s)
        with ExitStack() as ctx:
            s = semaphores(nc, ctx, ["chain", "bn_var", "bn_root", "scaled", "h_ready", "turned", "var_ready", "taken", "root_ready",
                               "rows_ready", "stored", "kept", "y_kept", "normed"], "batch")
            mv = ctx.enter_context(sbuf(nc, "bn_mv", [D, 8], F32))
            hs = ctx.enter_context(sbuf(nc, "hs", [D, SN], F32))
            h = ctx.enter_context(sbuf(nc, "h", [TN, ST, D], F32))
            normed = ctx.enter_context(sbuf(nc, "normed", [TN, ST, D], F32))
            rows = ctx.enter_context(sbuf(nc, "rows", [TN, ST, D], F32))
            ps_n = ctx.enter_context(psum(nc, "ps_n", [P, ST, D], F32))
            n = Norm(nc, ctx)
            with nc.Block() as block:
                @block.sync
                def _(sp):
                    store_steps(sp, s, table, rows[:, :, :])

                @block.scalar
                def _(act):
                    act.wait_ge(s["bn_var"], 1)
                    act.activation(mv[:, 2:3], mv[:, 1:2], ACT.Sqrt, bias=c.eps[0:D, 0:1]).then_inc(s["bn_root"], 1)
                    act.wait_ge(s["scaled"], 1)
                    def turn(t):
                        wait(act, s["turned"], t)
                        act.activation(hs[:, :], ht[:, span(t)], ACT.Relu, bias=mv[:, 6:7], scale=mv[:, 4:5])\
                            .then_inc(s["h_ready"], 1)
                        root_of_var(act, c, s, t, n)
                        act.wait_ge(s["normed"], t + 1)
                        act.activation(c.x_nodes[:, ds(t * ST, ST), :], normed[:, :, :], ACT.Copy).then_inc(s["kept"], 1)
                        act.wait_ge(s["rows_ready"], t + 1)
                        act.activation(c.y_nodes[:, ds(t * ST, ST), :], rows[:, :, :], ACT.Copy).then_inc(s["y_kept"], 1)

                    steps(act, turn)

                @block.tensor
                def _(pe):
                    def turn(t):
                        pe.wait_ge(s["h_ready"], t + 1)
                        wait(pe, s["normed"], t)
                        for k in range(ST):
                            ins = pe.transpose(ps_n[0:TN, k, :], hs[:, k * TN:(k + 1) * TN], c.ident[0:D, 0:D])
                        ins.then_inc(s["turned"], 1)

                    steps(pe, turn)

                @block.vector
                def _(dve):
                    ch = Chain(dve, s["bn_var"])
                    ch.then(dve.bn_aggr(mv[:, 0:2], stats[:, :, :].rearrange("p a b -> p (a b)")))
                    dve.wait_ge(s["bn_root"], 1)
                    ch.then(dve.reciprocal(mv[:, 3:4], mv[:, 2:3]))
                    ch.then(dve.tensor_tensor(mv[:, 4:5], mv[:, 3:4], c.gamma[:, :], ALU.mult))
                    ch.then(dve.tensor_tensor(mv[:, 5:6], mv[:, 0:1], mv[:, 4:5], ALU.mult))
                    dve.tensor_tensor(mv[:, 6:7], c.beta[:, :], mv[:, 5:6], ALU.subtract).then_inc(s["scaled"], 1)
                    def turn(t):
                        ch = Chain(dve, s["chain"], t, 3)
                        dve.wait_ge(s["turned"], t + 1)
                        ch.then(dve.tensor_tensor(h[:, :, :], ps_n[0:TN, :, :], c.x_nodes[:, ds(t * ST, ST), :], ALU.add))
                        wait(dve, s["kept"], t)
                        layer_norm(dve, ch, c, s, t, n, h, normed).then_inc(s["normed"], 1)
                        dve.wait_ge(s["normed"], t + 1)
                        wait(dve, s["stored"], t * 16)
                        wait(dve, s["y_kept"], t)
                        dve.tensor_tensor(rows[:, :, :], normed[:, :, :],
                                          c.dis[:, ds(t * ST, ST)].unsqueeze(2).to_broadcast([TN, ST, D]), ALU.mult)\
                            .then_inc(s["rows_ready"], 1)

                    steps(dve, turn)
            clear_semaphores(nc, s)


def degree_row(nc, c):
    with ExitStack() as ctx:
        s = semaphores(nc, ctx, ["turned", "copied", "moved"], "degree_row")
        turned = ctx.enter_context(sbuf(nc, "dis_turned", [TILES, TN], F32))
        ps = ctx.enter_context(psum(nc, "ps_dis", [P, 512], F32))
        with nc.Block() as block:
            @block.tensor
            def _(pe):
                pe.transpose(ps[0:TILES, 0:TN], c.dis[:, :], c.ident[0:TN, 0:TN]).then_inc(s["turned"], 1)

            @block.scalar
            def _(act):
                act.wait_ge(s["turned"], 1)
                act.activation(turned[:, :], ps[0:TILES, 0:TN], ACT.Copy).then_inc(s["copied"], 1)

            @block.sync
            def _(sp):
                sp.wait_ge(s["copied"], 1)
                sp.dma_start(c.sums[MROWS - 1:MROWS, 0:N], turned[:, :])\
                    .then_inc(s["moved"], 16)
                sp.wait_ge(s["moved"], 16)
        clear_semaphores(nc, s)


def after_first_convolution(nc, c, table):
    with ExitStack() as ctx:
        s = semaphores(nc, ctx, ["y_made", "turned", "dis_spread", "dis_ready", "s_ready", "local_done", "local_kept",
                           "g_done", "g_ready", "y_ready", "y_turned", "rows_ready", "stored", "chain"], "conv")
        ys = ctx.enter_context(sbuf(nc, "ys", [TN, ST, D], F32))
        dis = ctx.enter_context(sbuf(nc, "dis_step", [D, SN], F32))
        nb = ctx.enter_context(sbuf(nc, "nb_step", [D, SN], F32))
        g = ctx.enter_context(sbuf(nc, "g_step", [D, SN], F32))
        yt = ctx.enter_context(sbuf(nc, "yt_step", [D, SN], F32))
        rows = ctx.enter_context(sbuf(nc, "rows", [TN, ST, D], F32))
        ps_t = ctx.enter_context(psum(nc, "ps_t", [P, 1024], F32))
        ps_d = ctx.enter_context(psum(nc, "ps_d", [P, 1024], F32))
        ps_l = ctx.enter_context(psum(nc, "ps_l", [P, 1024], F32))
        ps_n = ctx.enter_context(psum(nc, "ps_n", [P, ST, D], F32))
        with nc.Block() as block:
            @block.sync
            def _(sp):
                store_steps(sp, s, table, rows[:, :, :])

            @block.tensor
            def _(pe):
                def turn(t):
                    wait(pe, s["dis_ready"], t)
                    for a, q, w in PIECES:
                        ins = pe.matmul(ps_d[0:D, q:q + w], c.count_row[0:MROWS, :], c.sums[0:MROWS, ds(t * SN + a, w)],
                                        start=True, stop=True)
                    ins.then_inc(s["dis_spread"], 1)
                    pe.wait_ge(s["y_made"], t + 1)
                    wait(pe, s["g_ready"], t)
                    for k in range(ST):
                        q = psum_tile_at(k)
                        ins = pe.transpose(ps_t[0:D, q:q + TN], ys[:, k, :], c.ident[0:TN, 0:TN])
                    ins.then_inc(s["turned"], 1)
                    pe.wait_ge(s["s_ready"], t + 1)
                    wait(pe, s["local_kept"], t)
                    for a, q, w in PIECES:
                        ins = pe.matmul(ps_l[0:D, q:q + w], c.w_local[:, :], nb[:, a:a + w], start=True, stop=True)
                    ins.then_inc(s["local_done"], 1)
                    for a, q, w in PIECES:
                        ins = pe.matmul(ps_t[0:D, q:q + w], c.w_g1[:, :], nb[:, a:a + w], start=True, stop=True)
                    ins.then_inc(s["g_done"], 1)
                    pe.wait_ge(s["y_ready"], t + 1)
                    wait(pe, s["rows_ready"], t)
                    for k in range(ST):
                        ins = pe.transpose(ps_n[0:TN, k, :], yt[:, k * TN:(k + 1) * TN], c.ident[0:D, 0:D])
                    ins.then_inc(s["y_turned"], 1)

                steps(pe, turn)

            @block.scalar
            def _(act):
                def turn(t):
                    act.wait_ge(s["dis_spread"], t + 1)
                    wait(act, s["y_ready"], t)
                    for a, q, w in PIECES:
                        ins = act.activation(dis[:, a:a + w], ps_d[0:D, q:q + w], ACT.Copy)
                    ins.then_inc(s["dis_ready"], 1)
                    act.wait_ge(s["local_done"], t + 1)
                    for a, q, w in PIECES:
                        ins = act.activation(c.local_t[:, ds(t * SN + a, w)], ps_l[0:D, q:q + w], ACT.Relu,
                                             bias=c.b_local[:, 0:1])
                    ins.then_inc(s["local_kept"], 1)
                    act.wait_ge(s["g_done"], t + 1)
                    for a, q, w in PIECES:
                        ins = act.activation(g[:, a:a + w], ps_t[0:D, q:q + w], ACT.Relu, bias=c.b_g1[:, 0:1])
                    ins.then_inc(s["g_ready"], 1)
                    act.wait_ge(s["y_turned"], t + 1)
                    wait(act, s["stored"], t * 16)
                    act.activation(rows[:, :, :], ps_n[0:TN, :, :], ACT.Copy)
                    act.activation(c.y_nodes[:, ds(t * ST, ST), :], ps_n[0:TN, :, :], ACT.Copy)\
                        .then_inc(s["rows_ready"], 1)

                steps(act, turn)

            @block.vector
            def _(dve):
                def turn(t):
                    ch = Chain(dve, s["chain"], t, 3)
                    wait(dve, s["turned"], t)
                    dve.tensor_tensor(ys[:, :, :], c.x_nodes[:, ds(t * ST, ST), :],
                                      c.dis[:, ds(t * ST, ST)].unsqueeze(2).to_broadcast([TN, ST, D]), ALU.mult)\
                        .then_inc(s["y_made"], 1)
                    dve.wait_ge(s["dis_ready"], t + 1)
                    dve.wait_ge(s["turned"], t + 1)
                    wait(dve, s["g_done"], t)
                    for a, q, w in PIECES:
                        ins = dve.tensor_tensor(nb[:, a:a + w], c.sums[0:D, ds(t * SN + a, w)], ps_t[0:D, q:q + w], ALU.add)
                    ch.then(ins)
                    dve.tensor_tensor(nb[:, :], nb[:, :], dis[:, :], ALU.mult).then_inc(s["s_ready"], 1)
                    dve.wait_ge(s["g_ready"], t + 1)
                    wait(dve, s["y_turned"], t)
                    ch.then(dve.tensor_tensor(yt[:, :], g[:, :], dis[:, :], ALU.mult))
                    dve.sem_inc(s["y_ready"], 1)
                    ch.then(dve.tensor_copy(c.y_t[:, span(t)], yt[:, :]))

                steps(dve, turn)
        clear_semaphores(nc, s)


def after_second_convolution(nc, c, table):
    with ExitStack() as ctx:
        s = semaphores(nc, ctx, ["dis_spread", "dis_ready", "s_ready", "g_done", "g_ready", "local_ready", "fused",
                           "var_ready", "taken", "root_ready", "rows_ready", "stored", "kept", "chain", "ones_made"], "fuse")
        dis = ctx.enter_context(sbuf(nc, "dis_step", [D, SN], F32))
        nb = ctx.enter_context(sbuf(nc, "nb_step", [D, SN], F32))
        g = ctx.enter_context(sbuf(nc, "g_step", [D, SN], F32))
        local = ctx.enter_context(sbuf(nc, "local_step", [D + 1, SN], F32))
        h = ctx.enter_context(sbuf(nc, "h", [TN, ST, D], F32))
        rows = ctx.enter_context(sbuf(nc, "rows", [TN, ST, D], F32))
        ps_d = ctx.enter_context(psum(nc, "ps_d", [P, 1024], F32))
        ps_g = ctx.enter_context(psum(nc, "ps_g", [P, 1024], F32))
        ps_n = ctx.enter_context(psum(nc, "ps_n", [P, ST, D], F32))
        n = Norm(nc, ctx)
        with nc.Block() as block:
            @block.sync
            def _(sp):
                store_steps(sp, s, table, rows[:, :, :])

            @block.tensor
            def _(pe):
                def turn(t):
                    wait(pe, s["dis_ready"], t)
                    for a, q, w in PIECES:
                        ins = pe.matmul(ps_d[0:D, q:q + w], c.count_row[0:MROWS, :], c.sums[0:MROWS, ds(t * SN + a, w)],
                                        start=True, stop=True)
                    ins.then_inc(s["dis_spread"], 1)
                    pe.wait_ge(s["s_ready"], t + 1)
                    wait(pe, s["g_ready"], t)
                    for a, q, w in PIECES:
                        ins = pe.matmul(ps_g[0:D, q:q + w], c.w_g2[:, :], nb[:, a:a + w], start=True, stop=True)
                    ins.then_inc(s["g_done"], 1)
                    pe.wait_ge(s["g_ready"], t + 1)
                    pe.wait_ge(s["local_ready"], t + 1)
                    pe.wait_ge(s["ones_made"], 1)
                    wait(pe, s["rows_ready"], t)
                    for k in range(ST):
                        at = slice(k * TN, (k + 1) * TN)
                        pe.matmul(ps_n[0:TN, k, :], local[:, at], c.w_f1[:, :], start=True, stop=False)
                        ins = pe.matmul(ps_n[0:TN, k, :], g[:, at], c.w_f2[:, :], start=False, stop=True)
                    ins.then_inc(s["fused"], 1)

                steps(pe, turn)

            @block.scalar
            def _(act):
                def turn(t):
                    wait(act, s["fused"], t)
                    act.activation(local[0:D, :], c.local_t[:, span(t)], ACT.Copy).then_inc(s["local_ready"], 1)
                    act.wait_ge(s["dis_spread"], t + 1)
                    wait(act, s["s_ready"], t)
                    for a, q, w in PIECES:
                        ins = act.activation(dis[:, a:a + w], ps_d[0:D, q:q + w], ACT.Copy)
                    ins.then_inc(s["dis_ready"], 1)
                    act.wait_ge(s["g_done"], t + 1)
                    for a, q, w in PIECES:
                        ins = act.activation(g[:, a:a + w], ps_g[0:D, q:q + w], ACT.Relu, bias=c.b_g2[:, 0:1])
                    ins.then_inc(s["g_ready"], 1)
                    root_of_var(act, c, s, t, n)
                    act.wait_ge(s["rows_ready"], t + 1)
                    act.activation(c.x_nodes[:, ds(t * ST, ST), :], rows[:, :, :], ACT.Copy).then_inc(s["kept"], 1)

                steps(act, turn)

            @block.vector
            def _(dve):
                dve.memset(local[D:D + 1, :], 1.0).then_inc(s["ones_made"], 1)
                def turn(t):
                    ch = Chain(dve, s["chain"], t, 4)
                    dve.wait_ge(s["dis_ready"], t + 1)
                    wait(dve, s["g_done"], t)
                    ch.then(dve.tensor_tensor(nb[:, :], c.sums[0:D, span(t)], c.y_t[:, span(t)], ALU.add))
                    dve.tensor_tensor(nb[:, :], nb[:, :], dis[:, :], ALU.mult).then_inc(s["s_ready"], 1)
                    dve.wait_ge(s["fused"], t + 1)
                    ch.then(dve.tensor_tensor(h[:, :, :], ps_n[0:TN, :, :], c.x_nodes[:, ds(t * ST, ST), :], ALU.add))
                    wait(dve, s["stored"], t * 16)
                    wait(dve, s["kept"], t)
                    layer_norm(dve, ch, c, s, t, n, h, rows).then_inc(s["rows_ready"], 1)

                steps(dve, turn)
        clear_semaphores(nc, s)


def after_edges(nc, c, out):
    with ExitStack() as ctx:
        s = semaphores(nc, ctx, ["x_copied", "turned", "s_ready", "h_done", "h_ready", "out_done", "var_ready", "taken", "root_ready",
                           "rows_ready", "stored", "chain", "ones_made"], "mlp")
        xs = ctx.enter_context(sbuf(nc, "xs", [TN, ST, D], F32))
        st = ctx.enter_context(sbuf(nc, "st", [D, SN], F32))
        hid = ctx.enter_context(sbuf(nc, "hid", [D + 1, SN], F32))
        h = ctx.enter_context(sbuf(nc, "h", [TN, ST, D], F32))
        rows = ctx.enter_context(sbuf(nc, "rows", [TN, ST, D], F32))
        ps_t = ctx.enter_context(psum(nc, "ps_t", [P, 1024], F32))
        ps_h = ctx.enter_context(psum(nc, "ps_h", [P, 1024], F32))
        ps_n = ctx.enter_context(psum(nc, "ps_n", [P, ST, D], F32))
        n = Norm(nc, ctx)
        with nc.Block() as block:
            @block.sync
            def _(sp):
                store_steps(sp, s, out, rows[:, :, :])

            @block.tensor
            def _(pe):
                def turn(t):
                    pe.wait_ge(s["x_copied"], t + 1)
                    wait(pe, s["s_ready"], t)
                    for k in range(ST):
                        q = psum_tile_at(k)
                        ins = pe.transpose(ps_t[0:D, q:q + TN], xs[:, k, :], c.ident[0:TN, 0:TN])
                    ins.then_inc(s["turned"], 1)
                    pe.wait_ge(s["s_ready"], t + 1)
                    wait(pe, s["h_ready"], t)
                    for a, q, w in PIECES:
                        ins = pe.matmul(ps_h[0:D, q:q + w], c.w_1[:, :], st[:, a:a + w], start=True, stop=True)
                    ins.then_inc(s["h_done"], 1)
                    pe.wait_ge(s["h_ready"], t + 1)
                    pe.wait_ge(s["ones_made"], 1)
                    wait(pe, s["rows_ready"], t)
                    for k in range(ST):
                        ins = pe.matmul(ps_n[0:TN, k, :], hid[:, k * TN:(k + 1) * TN], c.w_2[:, :], start=True, stop=True)
                    ins.then_inc(s["out_done"], 1)

                steps(pe, turn)

            @block.scalar
            def _(act):
                def turn(t):
                    wait(act, s["rows_ready"], t)
                    act.activation(xs[:, :, :], c.x_nodes[:, ds(t * ST, ST), :], ACT.Copy).then_inc(s["x_copied"], 1)
                    act.wait_ge(s["h_done"], t + 1)
                    for a, q, w in PIECES:
                        ins = act.activation(hid[0:D, a:a + w], ps_h[0:D, q:q + w], ACT.Relu, bias=c.b_1[:, 0:1])
                    ins.then_inc(s["h_ready"], 1)
                    root_of_var(act, c, s, t, n)

                steps(act, turn)

            @block.vector
            def _(dve):
                dve.memset(hid[D:D + 1, :], 1.0).then_inc(s["ones_made"], 1)
                def turn(t):
                    ch = Chain(dve, s["chain"], t, 4)
                    dve.wait_ge(s["turned"], t + 1)
                    wait(dve, s["h_done"], t)
                    for a, q, w in PIECES:
                        ins = dve.tensor_tensor(st[:, a:a + w], c.sums[0:D, ds(t * SN + a, w)], ps_t[0:D, q:q + w], ALU.add)
                    ins.then_inc(s["s_ready"], 1)
                    dve.wait_ge(s["out_done"], t + 1)
                    ch.then(dve.scalar_tensor_tensor(out=h[:, :, :], in0=ps_n[0:TN, :, :], scalar=0.0, in1=xs[:, :, :],
                                                     op0=ALU.max, op1=ALU.add))
                    ch.then(dve.tensor_tensor(h[:, :, :], h[:, :, :], xs[:, :, :], ALU.add))
                    wait(dve, s["stored"], t * 16)
                    layer_norm(dve, ch, c, s, t, n, h, rows).then_inc(s["rows_ready"], 1)

                steps(dve, turn)
        clear_semaphores(nc, s)


class Chip:

    def __init__(self, nc, ctx):
        def sb(name, shape, dt=F32):
            return ctx.enter_context(sbuf(nc, name, shape, dt))

        self.x_nodes = sb("x_nodes", [TN, TILES, D])
        self.sums = sb("sums", [P, NPAD])
        self.local_t = sb("local_t", [D, N])
        self.y_t = sb("y_t", [D, N])
        self.dst_f = sb("dst_f", [P, NB * COLS])
        self.rel = sb("rel", [P, (NB + 1) * COLS])
        self.first_dst = sb("first_dst", [P, NB])
        self.base_f = sb("base_f", [P, NB])
        self.base_i = sb("base_i", [P, NB], I32)
        self.round_base = sb("round_base", [P, 1])
        self.sorted_ = sb("all_inside", [P, 1])
        self.n_rounds = sb("n_rounds", [P, 1], I32)
        self.eps = sb("eps", [P, 1])
        self.deg = sb("deg", [TN, TILES])
        self.dis = sb("dis", [TN, TILES])
        self.iota = sb("iota", [P, WIN])
        self.ident = sb("ident", [P, P])
        self.count_row = sb("count_row", [P, D])
        self.w_kvq = sb("w_kvq", [D + 1, 3, D])
        self.w_e = sb("w_e", [D + 1, D])
        self.w_f1 = sb("w_f1", [D + 1, D])
        self.w_2 = sb("w_2", [D + 1, D])
        self.w_l = sb("w_l", [D, D])
        self.w_r = sb("w_r", [D, D])
        self.w_local = sb("w_local", [D, D])
        self.w_g1 = sb("w_g1", [D, D])
        self.w_g2 = sb("w_g2", [D, D])
        self.w_f2 = sb("w_f2", [D, D])
        self.w_1 = sb("w_1", [D, D])
        self.b_l = sb("b_l", [D, 1])
        self.gamma = sb("gamma", [D, 1])
        self.beta = sb("beta", [D, 1])
        self.b_local = sb("b_local", [D, 1])
        self.b_g1 = sb("b_g1", [D, 1])
        self.b_g2 = sb("b_g2", [D, 1])
        self.b_1 = sb("b_1", [D, 1])
        self.y_nodes = sb("y_nodes", [TN, TILES, D])
        self.starts = sb("starts", [1, GROUPS], I32)
        self.dense_f = sb("dense_f", [1, 4])
        self.dense = sb("dense", [1, 1], I32)
        self.edge_keys = nc.dram_tensor("edge_keys", [NB * EPB, 2], F32).ap()
        self.adjacency = nc.dram_tensor("adjacency", [CHUNKS, 2, TN, HALF * CHUNK], U8).ap()
        self.kv_table = nc.dram_tensor("kv_table", [N, 2 * D], F32).ap()
        self.q_table = nc.dram_tensor("q_table", [N + WIN, D], F32).ap()
        self.tables = [nc.dram_tensor(f"node_table{i}", [N, D], F32).ap() for i in range(4)]


def graph_layers(nc, A, out):
    with ExitStack() as ctx:
        c = Chip(nc, ctx)
        setup(nc, c, A)
        edge_keys(nc, c, A)
        project(nc, c, A)
        rounds = nc.values_load(c.n_rounds[0:1, 0:1], min_val=1, max_val=ROUNDS)

        def edges(kind, table):
            with nc.Fori(0, rounds):
                place_windows(nc, c)
                edge_pass(nc, c, A, kind, table)

        edges("attend", c.kv_table)
        group_starts(nc, c)
        build_adjacency(nc, c)
        dense = nc.values_load(c.dense[0:1, 0:1], min_val=0, max_val=1)

        def neighbours(rows, table):
            with nc.If(dense > 0):
                nc.all_engine_barrier()
                dense_pass(nc, c, rows)
            with nc.Else():
                nc.all_engine_barrier()
                clear_sums(nc, c)
                edges("plain", table)

        after_attention(nc, c, c.tables[0])
        neighbours(c.x_nodes, c.tables[0])
        after_mean(nc, c, c.tables[1])
        degree_row(nc, c)
        neighbours(c.y_nodes, c.tables[1])
        after_first_convolution(nc, c, c.tables[2])
        neighbours(c.y_nodes, c.tables[2])
        after_second_convolution(nc, c, c.tables[3])
        clear_sums(nc, c)
        edges("relu", c.tables[3])
        after_edges(nc, c, out)


ROWS = ("L0_gnn_bk", "L0_gnn_bv", "L0_gnn_bq", "L0_gnn_be", "L2_gnn_b_fuse", "L3_gnn_b2")
COLUMNS = ("L1_gnn_bl", "L1_gnn_gamma", "L1_gnn_beta", "L2_gnn_b_local", "L2_gnn_b_g1", "L2_gnn_b_g2", "L3_gnn_b1")


def kernel(**inputs):
    import numpy as np
    import concourse.bacc as bacc
    from concourse.bass_utils import run_bass_kernel_spmd

    arrays = {k: np.asarray(v) for k, v in inputs.items()}
    for k in ROWS:
        arrays[k] = arrays[k].reshape(1, D)
    for k in COLUMNS:
        arrays[k] = arrays[k].reshape(D, 1)
    for k in ("L1_gnn_Wl", "L1_gnn_Wr"):
        arrays[k + "T"] = arrays.pop(k).T
    for k, fill in (("src", 0), ("dst", -1)):
        padded = np.full(NB * EPB, fill, arrays[k].dtype)
        padded[:E] = arrays[k]
        arrays[k] = padded.reshape(NB, P, COLS)
    nc = bacc.Bacc("TRN2", target_bir_lowering=False, num_devices=1)
    aps = {}
    for k in arrays:
        arrays[k] = np.ascontiguousarray(arrays[k])
        aps[k] = nc.dram_tensor(k + "_in", arrays[k].shape, mybir.dt.from_np(arrays[k].dtype), kind="ExternalInput").ap()
    out = nc.dram_tensor("x_out", (N, D), F32, kind="ExternalOutput").ap()
    graph_layers(nc, aps, out)
    r = run_bass_kernel_spmd(nc, [{k + "_in": v for k, v in arrays.items()}], core_ids=[0])
    return r.results[0]["x_out"]
```
